# Optimizing a Trainium2 kernel written in Bass

```python
import numpy as np
import jax
import jax.numpy as jnp

def _softmax(x, axis=-1):
    return jax.nn.softmax(x, axis=axis)

def _gelu(x):
    return jax.nn.gelu(x, approximate=True)

def _silu(x):
    return jax.nn.silu(x)

def _sigmoid(x):
    return jax.nn.sigmoid(x)

def _layernorm(x, axis=-1, eps=1e-05):
    m = jnp.mean(x, axis=axis, keepdims=True)
    v = jnp.var(x, axis=axis, keepdims=True)
    return (x - m) / jnp.sqrt(v + eps)

def _scatter_add(tgt, idx, src, axis=0):
    return tgt.at[idx].add(src)

def _segment_sum(src, seg, n):
    return jax.ops.segment_sum(src, seg, n)
kernel_name = 'mk_decoder_preln_d1_seqx_r4_b1fb13'

def setup_inputs(seed: int=0):
    np.random.seed(seed)
    _w = jnp.asarray

    def _rec_inputs():
        import jax
        import jax.numpy as jnp
        _rk = jax.random.key(seed)
        x = -0.0003929 + 0.9999 * jax.random.normal(jax.random.fold_in(_rk, 1), (16, 128, 512), jnp.float32)
        _lenS = 128 - jax.random.randint(jax.random.fold_in(_rk, 7), (16,), 0, max(1, 128 // 4) + 1, jnp.int32)
        _lenS2 = 128 - jax.random.randint(jax.random.fold_in(_rk, 8), (16,), 0, max(1, 128 // 4) + 1, jnp.int32)
        _ctx_2048P = jax.random.normal(jax.random.fold_in(_rk, 11), (16, 16, 512), jnp.float32)
        _ctx_2048c = jax.random.dirichlet(jax.random.fold_in(_rk, 511), 0.3 * jnp.ones((16,), jnp.float32), (16, 128))
        _ctx_2048t = jnp.einsum('bsk,bkd->bsd', _ctx_2048c, _ctx_2048P)
        _ctx_2048t = _ctx_2048t * jax.lax.rsqrt(jnp.mean(jnp.square(_ctx_2048t)) + 1e-12) * 0.953939
        ctx_2048 = -0.000514642 + 1.00011 * (_ctx_2048t + 0.3 * jax.random.normal(jax.random.fold_in(_rk, 611), (16, 128, 512), jnp.float32))
        _validS = jnp.arange(128)[None, :] < _lenS[:, None]
        _validS2 = jnp.arange(128)[None, :] < _lenS2[:, None]
        _causal = jnp.tril(jnp.ones((128, 128), dtype=bool))
        mask_BxS2_ik0 = jnp.where(jnp.broadcast_to(_validS2[:, :], (16, 128)), 0, 1).astype(jnp.int32)
        return (x, ctx_2048, mask_BxS2_ik0)
    x, ctx_2048, mask_BxS2_ik0 = _rec_inputs()

    def _L0_attn_setup():
        import jax, jax.numpy as jnp
        import numpy as np
        import math
        HIDDEN = 512
        NUM_HEADS = 16
        HEAD_SIZE = HIDDEN // NUM_HEADS
        BATCH = 2
        SEQ = 512
        key = jax.random.key(seed)
        k_x, k_wq, k_bq, k_wo, k_bo = jax.random.split(key, 5)
        scale_in = 1.0 / math.sqrt(HIDDEN)
        return {'x': jax.random.normal(k_x, (BATCH, SEQ, HIDDEN), dtype=jnp.float32), 'Wqkv': jax.random.normal(k_wq, (HIDDEN, 3 * HIDDEN), dtype=jnp.float32) * scale_in, 'bqkv': jax.random.normal(k_bq, (3 * HIDDEN,), dtype=jnp.float32) * 0.01, 'Wo': jax.random.normal(k_wo, (HIDDEN, HIDDEN), dtype=jnp.float32) * scale_in, 'bo': jax.random.normal(k_bo, (HIDDEN,), dtype=jnp.float32) * 0.01}
    _L0_attn_all = _L0_attn_setup()
    _L0_attn_in = {k: v for k, v in _L0_attn_all.items() if k in ('Wqkv', 'bqkv', 'Wo', 'bo')}
    del _L0_attn_all

    def _L0_xattn_setup():
        import jax, jax.numpy as jnp
        import numpy as np
        import math
        H = 512
        NH = 16
        HD = H // NH
        EPS_LN = 1e-05
        RES_SCALE_MAX = 0.3

        def _nan_clean(x, lim=10000.0):
            return jnp.nan_to_num(x, nan=0.0, posinf=lim, neginf=-lim)
        key = jax.random.key(seed)
        ks = jax.random.split(key, 12)
        B, S, T = (4, 512, 64)
        std = 1.0 / math.sqrt(H)
        return {'hidden_states': jax.random.normal(ks[0], (B, S, H), jnp.float32), 'audio_tokens': jax.random.normal(ks[1], (B, T, H), jnp.float32), 'attention_mask': jax.random.randint(ks[2], (B, T), 0, 2, jnp.int32), 'Wq': jax.random.normal(ks[3], (H, H), jnp.float32) * std, 'bq': jnp.zeros((H,), jnp.float32), 'Wk': jax.random.normal(ks[4], (H, H), jnp.float32) * std, 'bk': jnp.zeros((H,), jnp.float32), 'Wv': jax.random.normal(ks[5], (H, H), jnp.float32) * std, 'bv': jnp.zeros((H,), jnp.float32), 'Wo': jax.random.normal(ks[6], (H, H), jnp.float32) * std, 'bo': jnp.zeros((H,), jnp.float32), 'ln_gamma': jnp.ones((H,), jnp.float32), 'ln_beta': jnp.zeros((H,), jnp.float32), 'residual_scale': jnp.float32(0.05)}
    _L0_xattn_all = _L0_xattn_setup()
    _L0_xattn_in = {k: v for k, v in _L0_xattn_all.items() if k in ('Wq', 'bq', 'Wk', 'bk', 'Wv', 'bv', 'Wo', 'bo', 'ln_gamma', 'ln_beta', 'residual_scale')}
    del _L0_xattn_all

    def _L0_ffn_setup():
        import jax, jax.numpy as jnp
        import numpy as np
        TOP_K = 6
        N_GROUP = 8
        TOPK_GROUP = 3
        CAPACITY = 192
        RSF = 1.0
        key = jax.random.key(seed)
        ks = jax.random.split(key, 8)
        B, S, H = (1, 1024, 512)
        E, M = (64, 352)
        MS = 704
        sc = 0.02
        return {'hidden_states': jax.random.normal(ks[0], (B, S, H), jnp.float32), 'gate_weight': jax.random.normal(ks[1], (E, H), jnp.float32) * sc, 'Wg': jax.random.normal(ks[2], (E, M, H), jnp.float32) * sc, 'Wu': jax.random.normal(ks[3], (E, M, H), jnp.float32) * sc, 'Wd': jax.random.normal(ks[4], (E, H, M), jnp.float32) * sc, 'Sg': jax.random.normal(ks[5], (MS, H), jnp.float32) * sc, 'Su': jax.random.normal(ks[6], (MS, H), jnp.float32) * sc, 'Sd': jax.random.normal(ks[7], (H, MS), jnp.float32) * sc}
    _L0_ffn_all = _L0_ffn_setup()
    _L0_ffn_in = {k: v for k, v in _L0_ffn_all.items() if k in ('gate_weight', 'Wg', 'Wu', 'Wd', 'Sg', 'Su', 'Sd')}
    del _L0_ffn_all
    return {'x': x, 'ctx_2048': ctx_2048, 'mask_BxS2_ik0': mask_BxS2_ik0, 'L0_attn_Wqkv': _L0_attn_in['Wqkv'], 'L0_attn_bqkv': _L0_attn_in['bqkv'], 'L0_attn_Wo': _L0_attn_in['Wo'], 'L0_attn_bo': _L0_attn_in['bo'], 'L0_xattn_Wq': _L0_xattn_in['Wq'], 'L0_xattn_bq': _L0_xattn_in['bq'], 'L0_xattn_Wk': _L0_xattn_in['Wk'], 'L0_xattn_bk': _L0_xattn_in['bk'], 'L0_xattn_Wv': _L0_xattn_in['Wv'], 'L0_xattn_bv': _L0_xattn_in['bv'], 'L0_xattn_Wo': _L0_xattn_in['Wo'], 'L0_xattn_bo': _L0_xattn_in['bo'], 'L0_xattn_ln_gamma': _L0_xattn_in['ln_gamma'], 'L0_xattn_ln_beta': _L0_xattn_in['ln_beta'], 'L0_xattn_residual_scale': _L0_xattn_in['residual_scale'], 'L0_ffn_gate_weight': _L0_ffn_in['gate_weight'], 'L0_ffn_Wg': _L0_ffn_in['Wg'], 'L0_ffn_Wu': _L0_ffn_in['Wu'], 'L0_ffn_Wd': _L0_ffn_in['Wd'], 'L0_ffn_Sg': _L0_ffn_in['Sg'], 'L0_ffn_Su': _L0_ffn_in['Su'], 'L0_ffn_Sd': _L0_ffn_in['Sd']}

def reference(x, ctx_2048, mask_BxS2_ik0, L0_attn_Wqkv, L0_attn_bqkv, L0_attn_Wo, L0_attn_bo, L0_xattn_Wq, L0_xattn_bq, L0_xattn_Wk, L0_xattn_bk, L0_xattn_Wv, L0_xattn_bv, L0_xattn_Wo, L0_xattn_bo, L0_xattn_ln_gamma, L0_xattn_ln_beta, L0_xattn_residual_scale, L0_ffn_gate_weight, L0_ffn_Wg, L0_ffn_Wu, L0_ffn_Wd, L0_ffn_Sg, L0_ffn_Su, L0_ffn_Sd):
    import jax
    import jax.numpy as jnp

    def _L0_attn_ref(x, Wqkv, bqkv, Wo, bo):
        import jax, jax.numpy as jnp
        import numpy as np
        import math
        HIDDEN = 512
        NUM_HEADS = 16
        HEAD_SIZE = HIDDEN // NUM_HEADS
        BATCH = 2
        SEQ = 512
        b, s, _ = x.shape
        kqv = x @ Wqkv + bqkv
        kqv = kqv.reshape(b, s, 3, NUM_HEADS, HEAD_SIZE)
        q = kqv[:, :, 0]
        k = kqv[:, :, 1]
        v = kqv[:, :, 2]
        scores = jnp.einsum('bsnh,btnh->bnst', k, q) / math.sqrt(HEAD_SIZE)
        ones = jnp.ones_like(scores)
        scores = jnp.triu(scores) + -10000.0 * jnp.tril(ones, k=-1)
        attn = jax.nn.softmax(scores, axis=2)
        out = jnp.einsum('bnkq,bknh->bqnh', attn, v)
        out = out.reshape(b, s, NUM_HEADS * HEAD_SIZE)
        return out @ Wo + bo

    def _L0_xattn_ref(hidden_states, audio_tokens, attention_mask, Wq, bq, Wk, bk, Wv, bv, Wo, bo, ln_gamma, ln_beta, residual_scale):
        import jax, jax.numpy as jnp
        import numpy as np
        import math
        H = 512
        NH = 16
        HD = H // NH
        EPS_LN = 1e-05
        RES_SCALE_MAX = 0.3

        def _nan_clean(x, lim=10000.0):
            return jnp.nan_to_num(x, nan=0.0, posinf=lim, neginf=-lim)
        B, S, _ = hidden_states.shape
        T = audio_tokens.shape[1]
        hs = _nan_clean(hidden_states).astype(jnp.float32)
        at = _nan_clean(audio_tokens).astype(jnp.float32)

        def proj(x, W, b, L):
            y = x @ W.T + b
            return y.reshape(B, L, NH, HD).transpose(0, 2, 1, 3)
        q = _nan_clean(proj(hs, Wq, bq, S))
        k = _nan_clean(proj(at, Wk, bk, T))
        v = _nan_clean(proj(at, Wv, bv, T))
        scale = max(math.sqrt(HD), 1e-08)
        scores = jnp.einsum('bhsd,bhtd->bhst', q, k) / scale
        scores = jnp.clip(scores, -50.0, 50.0)
        scores = jnp.nan_to_num(scores, nan=0.0, posinf=50.0, neginf=-50.0)
        attend = (attention_mask.astype(jnp.float32) > 0.5)[:, None, None, :]
        scores = jnp.where(attend, scores, -10000.0)
        scores = jnp.clip(scores, -50.0, 50.0)
        probs = jax.nn.softmax(scores, axis=-1)
        probs = jnp.nan_to_num(probs, nan=0.0, posinf=1.0, neginf=0.0)
        probs = probs / (probs.sum(axis=-1, keepdims=True) + 1e-08)
        ctx = jnp.einsum('bhst,bhtd->bhsd', probs, v)
        ctx = ctx.transpose(0, 2, 1, 3).reshape(B, S, H)
        delta = _nan_clean(ctx @ Wo.T + bo)
        rs = jnp.clip(residual_scale, 0.0, RES_SCALE_MAX)
        delta = rs * delta
        mu = delta.mean(axis=-1, keepdims=True)
        var = jnp.mean((delta - mu) ** 2, axis=-1, keepdims=True)
        delta = (delta - mu) / jnp.sqrt(var + EPS_LN) * ln_gamma + ln_beta
        return delta

    def _L0_ffn_ref(hidden_states, gate_weight, Wg, Wu, Wd, Sg, Su, Sd):
        import jax, jax.numpy as jnp
        import numpy as np
        TOP_K = 6
        N_GROUP = 8
        TOPK_GROUP = 3
        CAPACITY = 192
        RSF = 1.0
        B, S, H = hidden_states.shape
        E, M, _ = Wg.shape
        K, NG, TG, C = (TOP_K, N_GROUP, TOPK_GROUP, CAPACITY)
        x = hidden_states.reshape(-1, H)
        T = x.shape[0]
        logits = x.astype(jnp.float32) @ gate_weight.astype(jnp.float32).T
        scores = jax.nn.softmax(logits, axis=-1)
        group_scores = scores.reshape(T, NG, E // NG).max(axis=-1)
        _, gidx = jax.lax.top_k(group_scores, TG)
        gmask = jnp.zeros((T, NG), scores.dtype).at[jnp.arange(T)[:, None], gidx].set(1.0)
        smask = jnp.repeat(gmask, E // NG, axis=1)
        tmp_scores = jnp.where(smask > 0, scores, 0.0)
        topk_w, topk_i = jax.lax.top_k(tmp_scores, K)
        topk_w = topk_w * RSF
        flat = topk_i.reshape(-1)
        oh = jax.nn.one_hot(flat, E, dtype=jnp.int32)
        pos = jnp.sum(jnp.cumsum(oh, axis=0) * oh, axis=-1) - 1
        slot = flat * C + jnp.minimum(pos, C - 1)
        tok = jnp.arange(T * K) // K
        buf = jnp.zeros((E * C, H), x.dtype).at[slot].set(x[tok]).reshape(E, C, H)
        g = jnp.einsum('ech,emh->ecm', buf, Wg)
        u = jnp.einsum('ech,emh->ecm', buf, Wu)
        out = jnp.einsum('ecm,ehm->ech', jax.nn.silu(g) * u, Wd).reshape(E * C, H)
        yk = out[slot].reshape(T, K, H)
        y = jnp.sum(yk * topk_w[..., None].astype(yk.dtype), axis=1)
        shared = jax.nn.silu(x @ Sg.T) * (x @ Su.T) @ Sd.T
        return (y + shared).reshape(B, S, H)
    x = x + _L0_attn_ref(_layernorm(x, axis=-1), L0_attn_Wqkv, L0_attn_bqkv, L0_attn_Wo, L0_attn_bo)
    x = x + _L0_xattn_ref(_layernorm(x, axis=-1), ctx_2048, mask_BxS2_ik0, L0_xattn_Wq, L0_xattn_bq, L0_xattn_Wk, L0_xattn_bk, L0_xattn_Wv, L0_xattn_bv, L0_xattn_Wo, L0_xattn_bo, L0_xattn_ln_gamma, L0_xattn_ln_beta, L0_xattn_residual_scale)
    x = x + _L0_ffn_ref(_layernorm(x, axis=-1), L0_ffn_gate_weight, L0_ffn_Wg, L0_ffn_Wu, L0_ffn_Wd, L0_ffn_Sg, L0_ffn_Su, L0_ffn_Sd)
    return x

_drawn_inputs = setup_inputs


def setup_inputs(seed=0):
    import zlib

    import numpy as np

    out = dict(_drawn_inputs(seed))
    spreads = {'L0_xattn_bq': (0.0, 0.27),
     'L0_xattn_bk': (0.0, 2.0),
     'L0_xattn_bv': (0.0, 0.1),
     'L0_xattn_bo': (0.0, 0.1),
     'L0_xattn_ln_gamma': (1.0, 0.2),
     'L0_xattn_ln_beta': (0.0, 0.1)}
    factors = {'L0_attn_bqkv': 6.877,
     'L0_attn_bo': 7.664,
     'L0_ffn_gate_weight': 8.0,
     'L0_ffn_Wg': 8.0,
     'L0_ffn_Wu': 8.0,
     'L0_ffn_Wd': 8.0,
     'L0_ffn_Sg': 8.0,
     'L0_ffn_Su': 8.0,
     'L0_ffn_Sd': 8.0}
    for name, (base, spread) in spreads.items():
        noise = np.random.default_rng([zlib.crc32(name.encode()), seed]).standard_normal(out[name].shape)
        drawn = base * np.exp(spread * noise) if base else spread * noise
        out[name] = jnp.asarray(drawn.astype(out[name].dtype))
    for name, factor in factors.items():
        out[name] = (out[name] * factor).astype(out[name].dtype)
    return out
```

```python
import concourse.bass as bass
from concourse import mybir
from contextlib import ExitStack

F32 = mybir.dt.float32
F32R = mybir.dt.float32r
BF16 = mybir.dt.bfloat16
I32 = mybir.dt.int32
U32 = mybir.dt.uint32
ALU = mybir.AluOpType
ACT = mybir.ActivationFunctionType
AX = mybir.AxisListType.X

P = 128
BATCH, SEQ, H = 16, 128, 512
T = BATCH * SEQ
KC = H // P
NH, HD = 16, 32
HPC = P // HD
SCALE = float(HD) ** -0.5
LN_EPS = 1e-5
LANES = 2
PAIRS = BATCH // LANES
E, TOPK, GROUPS, TOPG = 64, 6, 8, 3
GSIZE = E // GROUPS
CAP = 192
SLOTS = E * CAP
NEG = -10000.0
CLIP = 50.0
RES_MAX = 0.3


class Chain:

    def __init__(self, eng, sem, per=0):
        self.eng, self.sem, self.per, self.base, self.n = eng, sem, per, 0, 0

    def turn(self, i, before):
        self.base, self.n = i * self.per + before, 0

    def link(self, ins):
        self.n += 1
        ins.then_inc(self.sem, 1)
        self.eng.wait_ge(self.sem, self.base + self.n)


def matmul3(pe, out, a, b, first, last):
    (ah, al), (bh, bl) = a, b
    pe.matmul(out, al, bh, start=first, stop=False)
    pe.matmul(out, ah, bl, start=False, stop=False)
    return pe.matmul(out, ah, bh, start=False, stop=last)


def transpose4(pe, bank, src, ident):
    for c in range(KC):
        ins = pe.transpose(bank[:, c * P:(c + 1) * P], src[:, c * P:(c + 1) * P], ident)
    return ins


def end_phase(nc, sems):
    nc.clear_and_free_semaphores(sems)
    nc.all_engine_barrier()


def attention_phase(nc, cross, x_in, ctx_in, w_in, w_out, vecs, out_x, route=None, const=None):
    ident = const["ident"]
    with ExitStack() as ctx:
        tag = "c_" if cross else "s_"

        def sb(name, shape, dt=F32):
            return ctx.enter_context(nc.sbuf_tensor(tag + name, shape, dt))

        sems = []

        def sem(name):
            sems.append(nc.alloc_semaphore(tag + name))
            return sems[-1]

        def lanes(make, name, *a):
            return [make(f"{name}{L}", *a) for L in range(LANES)]

        ps = [ctx.enter_context(nc.psum_tensor(f"{tag}ps{L}", [P, 4, 512], F32)) for L in range(LANES)]

        wi = [sb("wi_hi", [P, KC, 3 * H], F32R), sb("wi_lo", [P, KC, 3 * H], F32R)]
        wo = [sb("wo_hi", [P, KC, H], F32R), sb("wo_lo", [P, KC, H], F32R)]
        stage = sb("stage", [P, 2, H])
        bias_in = sb("bias_in", [P, 3 * H])
        bias_out = sb("bias_out", [P, H])
        minus_half = sb("minus_half", [P, 1])
        ready_mark = sb("ready_mark", [P, 1])
        scratch = sb("scratch", [P, 1])
        scratch_p = sb("scratch_p", [P, LANES])
        eps = sb("eps", [P, 1])
        if cross:
            gate = [sb("gate_hi", [P, KC, E], F32R), sb("gate_lo", [P, KC, E], F32R)]
            gamma = sb("gamma", [P, H])
            beta = sb("beta", [P, H])
            rs = sb("rs", [P, 1])
            rs2 = sb("rs2", [P, 1])
            nmask = sb("nmask", [P, T])
            imask = stage[:].rearrange("p a h -> p (a h)").bitcast(I32)
            IM = 2 * H
            iota8 = sb("iota8", [P, GROUPS])
            iota64 = sb("iota64", [P, E])
            before_me = sb("before_me", [P, P], BF16)
            all_ones = sb("all_ones", [P, P], BF16)
            diag_pos = sb("diag_pos", [P, P], BF16)
            rowid = sb("rowid", [P, 1])
            token = lanes(sb, "token", [P, 1])
            dump = lanes(sb, "dump", [P, TOPK])
            tbase = lanes(sb, "tbase", [E, 1])
            count = sb("count", [P, E])
            last_tok = sb("last_tok", [E, 1])
            zero_row = sb("zero_row", [E, CAP])
            gmax = lanes(sb, "gmax", [P, GROUPS])
            gtop = lanes(sb, "gtop", [P, 8])
            gidx = lanes(sb, "gidx", [P, 8], U32)
            gidf = lanes(sb, "gidf", [P, 8])
            gone = lanes(sb, "gone", [P, TOPG, GROUPS])
            gmask = lanes(sb, "gmask", [P, GROUPS])
            lneg = lanes(sb, "lneg", [P, 1])
            lsum = lanes(sb, "lsum", [P, 1])
            prob = lanes(sb, "prob", [P, E])
            top = lanes(sb, "top", [P, 8])
            tidx = lanes(sb, "tidx", [P, 8], U32)
            tidf = lanes(sb, "tidf", [P, 8])
            onehot = lanes(sb, "onehot", [P, TOPK, E])
            chosen = lanes(sb, "chosen", [P, E], BF16)
            posn = lanes(sb, "posn", [P, E])
            posk = lanes(sb, "posk", [P, TOPK])
            over = lanes(sb, "over", [P, TOPK])
            slot = lanes(sb, "slot", [P, TOPK])
            wslot = lanes(sb, "wslot", [P, TOPK], U32)
            lmax = lanes(sb, "lmax", [E, 1])
            lpos = lanes(sb, "lpos", [E, 1])
        else:
            tri_scale = sb("tri_scale", [P, P])
            tri_neg = sb("tri_neg", [P, P])

        x_sb = lanes(sb, "x", [P, H])
        xn = lanes(sb, "xn", [P, H])
        stats = lanes(sb, "stats", [P, 6])
        mv = lanes(sb, "mv", [P, 2])
        rstd = lanes(sb, "rstd", [P, 1])
        xnT = [[sb(f"xnT_hi{L}", [P, H], F32R), sb(f"xnT_lo{L}", [P, H], F32R)] for L in range(LANES)]
        q_sb = lanes(sb, "q", [P, H])
        k_sb = lanes(sb, "k", [P, H])
        v_sb = lanes(sb, "v", [P, NH, HD + 1])
        qT = lanes(sb, "qT", [P, H])
        kbd = lanes(sb, "kbd", [P, KC, HPC, SEQ])
        prb = lanes(sb, "prb", [P, NH, SEQ])
        nmax = lanes(sb, "nmax", [P, NH])
        rsum = lanes(sb, "rsum", [P, NH])
        rsum2 = lanes(sb, "rsum2", [P, NH])
        attn = lanes(sb, "attn", [P, H])
        aT = [[sb(f"aT_hi{L}", [P, H], F32R), sb(f"aT_lo{L}", [P, H], F32R)] for L in range(LANES)]
        xb = lanes(sb, "xb", [P, H])
        x1 = lanes(sb, "x1", [P, H])
        if cross:
            ctx_sb = lanes(sb, "ctx", [P, H])
            cT = [[sb(f"cT_hi{L}", [P, H], F32R), sb(f"cT_lo{L}", [P, H], F32R)] for L in range(LANES)]
            dlt = lanes(sb, "dlt", [P, H])
            fac = lanes(sb, "fac", [P, 1])
            xf = lanes(sb, "xf", [P, H])
            xfT = xnT

        s_vec = sem("vec_loaded")
        s_stage = [sem("stage_loaded0"), sem("stage_loaded1")]
        s_hi = sem("weight_hi")
        s_lo = sem("weight_lo")
        s_const = sem("const_ready")
        s_x = lanes(sem, "x_loaded")
        s_var = lanes(sem, "var_ready")
        s_rstd = lanes(sem, "rstd_ready")
        s_xn = lanes(sem, "xn_ready")
        s_xb = lanes(sem, "xb_ready")
        s_t1 = lanes(sem, "xnT_in_psum")
        s_t1h = lanes(sem, "xnT_hi_ready")
        s_t1l = lanes(sem, "xnT_lo_ready")
        s_m1 = lanes(sem, "qkv_in_psum")
        s_qk = lanes(sem, "qk_ready")
        s_v = lanes(sem, "v_ready")
        s_t2 = lanes(sem, "qkT_in_psum")
        s_qT = lanes(sem, "qT_ready")
        s_kbd = lanes(sem, "kbd_ready")
        s_sc = lanes(sem, "scores_in_psum")
        s_max = lanes(sem, "masked_ready")
        s_exp = lanes(sem, "exp_ready")
        s_pT = lanes(sem, "probsT_in_psum")
        s_pTs = lanes(sem, "probsT_ready")
        s_pv = lanes(sem, "pv_in_psum")
        s_at = lanes(sem, "attn_ready")
        s_t4 = lanes(sem, "attnT_in_psum")
        s_t4h = lanes(sem, "attnT_hi_ready")
        s_t4l = lanes(sem, "attnT_lo_ready")
        s_o = lanes(sem, "o_in_psum")
        s_of = lanes(sem, "o_bank_free")
        s_x1 = lanes(sem, "x1_ready")
        s_st = lanes(sem, "x1_stored")
        s_dve = sem("dve_step")
        s_pool = sem("pool_step")
        if cross:
            s_c = lanes(sem, "ctx_loaded")
            s_ch = lanes(sem, "ctx_hi_ready")
            s_cl = lanes(sem, "ctx_lo_ready")
            s_var2 = lanes(sem, "delta_var_ready")
            s_fac = lanes(sem, "delta_factor_ready")
            s_dn = lanes(sem, "delta_normed")
            s_var3 = lanes(sem, "x3_var_ready")
            s_rstd3 = lanes(sem, "x3_rstd_ready")
            s_xf = lanes(sem, "xf_ready")
            s_stf = lanes(sem, "xf_stored")
            s_t5 = lanes(sem, "xfT_in_psum")
            s_t5h = lanes(sem, "xfT_hi_ready")
            s_t5l = lanes(sem, "xfT_lo_ready")
            s_lg = lanes(sem, "logits_in_psum")
            s_lm = lanes(sem, "logit_max_ready")
            s_le = lanes(sem, "logit_exp_ready")
            s_choice = lanes(sem, "choice_ready")
            s_pos = lanes(sem, "positions_in_psum")
            s_posd = lanes(sem, "positions_read")
            s_ws = lanes(sem, "write_slots_ready")
            s_sct = lanes(sem, "tokens_scattered")
            s_mask = sem("mask_loaded")
            s_nm = sem("mask_ready")
            s_last = sem("last_tokens_ready")
            s_lst = sem("last_tokens_stored")

        pieces = []
        for src, hilo, col in w_in + [(w_out, wo, 0)] + ([(route["gate"], gate, 0)] if cross else []):
            dst = wi if hilo is None else hilo
            n = src.shape[1]
            for k in range(KC):
                for a in range(0, n, H):
                    m = min(H, n - a)
                    pieces.append((src[k * P:(k + 1) * P, a:a + m], [d[:, k, col + a:col + a + m] for d in dst], m))

        ctx.callback(end_phase, nc, sems)
        block = ctx.enter_context(nc.Block())

        @block.sync
        def _(sp):
            def load(i, L):
                b = i * LANES + L
                sp.dma_start(x_sb[L][:], x_in[bass.ds(b * P, P), :]).then_inc(s_x[L], 16)
                if cross:
                    sp.dma_start(ctx_sb[L][:], ctx_in[bass.ds(b * P, P), :]).then_inc(s_c[L], 16)

            def load_next(i, L):
                sp.wait_ge(s_xn[L], i + 1)
                sp.wait_ge(s_xb[L], i + 1)
                if cross:
                    sp.wait_ge(s_cl[L], i + 1)
                load(i + 1, L)

            def store(i, L):
                b = i * LANES + L
                sp.wait_ge(s_x1[L], i + 1)
                sp.dma_start(out_x[bass.ds(b * P, P), :], x1[L][:]).then_inc(s_st[L], 16)
                if cross:
                    sp.wait_ge(s_xf[L], i + 1)
                    sp.dma_start(route["xf"][bass.ds(b * P, P), :], xf[L][:]).then_inc(s_stf[L], 16)

            for L in range(LANES):
                load(0, L)
            for n, (src, dst, m) in enumerate(pieces):
                if n >= 2:
                    sp.wait_ge(s_lo, n - 1)
                sp.dma_start(stage[:, n % 2, 0:m], src).then_inc(s_stage[n % 2], 16)
            if cross:
                sp.wait_ge(s_lo, len(pieces))
                for n in range(T // IM):
                    if n:
                        sp.wait_ge(s_nm, n)
                    sp.dma_start(imask, route["mask"][n * IM:(n + 1) * IM].partition_broadcast(P)).then_inc(s_mask, 16)
            with sp.Fori(0, PAIRS - 1) as i:
                for L in range(LANES):
                    load_next(i, L)
                for L in range(LANES):
                    store(i, L)
            for L in range(LANES):
                store(PAIRS - 1, L)
            if cross:
                sp.wait_ge(s_last, 1)
                for L in range(LANES):
                    sp.wait_ge(s_sct[L], 16 + 16 * TOPK * PAIRS)
                table = route["table"][0:SLOTS, :].rearrange("(e c) o -> e (c o)", c=CAP)
                sp.dma_start(table[:, CAP - 1:CAP], last_tok[:], allow_slow_non_contiguous=True).then_inc(s_lst, 16)
                sp.wait_ge(s_lst, 16)
            for L in range(LANES):
                sp.wait_ge(s_st[L], 16 * PAIRS)
                if cross:
                    sp.wait_ge(s_stf[L], 16 * PAIRS)

        @block.gpsimd
        def _(pool):
            chain = Chain(pool, s_pool)
            if cross:
                n = 0
                for src, dst in zip(vecs[:6], (bias_in[:, 0:H], bias_in[:, H:2 * H], bias_in[:, 2 * H:3 * H],
                                               bias_out[:], gamma[:], beta[:])):
                    pool.dma_start(dst, src.partition_broadcast(P)).then_inc(s_vec, 16)
                    n += 1
                pool.dma_start(rs[:], vecs[6].partition_broadcast(P)).then_inc(s_vec, 16)
                n += 1
            else:
                for src, dst in zip(vecs, (bias_in[:], bias_out[:])):
                    pool.dma_start(dst, src.partition_broadcast(P)).then_inc(s_vec, 16)
                n = len(vecs)
            nvec = n
            chain.link(pool.memset(minus_half[:], -0.5))
            chain.link(pool.memset(eps[:], LN_EPS))
            for L in range(LANES):
                chain.link(pool.memset(kbd[L][:], 0.0))
                chain.link(pool.memset(v_sb[L][:, :, HD:HD + 1], 1.0))
            if not cross:
                chain.link(pool.memset(ident[:], 0.0))
                chain.link(pool.affine_select(out=ident[:], in_=ident[:], pattern=[[-1, P]], compare_op=ALU.not_equal,
                                              fill=1.0, base=0, channel_multiplier=1))
                chain.link(pool.memset(tri_scale[:], SCALE))
                chain.link(pool.affine_select(out=tri_scale[:], in_=tri_scale[:], pattern=[[-1, P]],
                                              compare_op=ALU.is_ge, fill=0.0, base=0, channel_multiplier=1))
                chain.link(pool.memset(tri_neg[:], 0.0))
                chain.link(pool.affine_select(out=tri_neg[:], in_=tri_neg[:], pattern=[[-1, P]],
                                              compare_op=ALU.is_ge, fill=NEG, base=0, channel_multiplier=1))
            else:
                lk = chain.link
                lk(pool.iota(iota8[:], pattern=[[1, GROUPS]], base=0, channel_multiplier=0,
                             allow_small_or_imprecise_dtypes=True))
                lk(pool.iota(iota64[:], pattern=[[1, E]], base=0, channel_multiplier=0,
                             allow_small_or_imprecise_dtypes=True))
                lk(pool.memset(all_ones[:], 1.0))
                lk(pool.affine_select(out=before_me[:], in_=all_ones[:], pattern=[[1, P]],
                                      compare_op=ALU.is_gt, fill=0.0, base=0, channel_multiplier=-1))
                lk(pool.iota(diag_pos[:], pattern=[[1, P]], base=1, channel_multiplier=0,
                             allow_small_or_imprecise_dtypes=True))
                lk(pool.affine_select(out=diag_pos[:], in_=diag_pos[:], pattern=[[1, P]],
                                      compare_op=ALU.is_equal, fill=0.0, base=0, channel_multiplier=-1))
                lk(pool.memset(count[:], 0.0))
                lk(pool.memset(last_tok[:], 0.0))
                lk(pool.memset(zero_row[:], 0.0))
                for L in range(LANES):
                    lk(pool.iota(token[L][:], pattern=[[0, 1]], base=(L - LANES) * P, channel_multiplier=1,
                                 allow_small_or_imprecise_dtypes=True))
                    lk(pool.iota(dump[L][:], pattern=[[1, TOPK]], base=SLOTS + (L - LANES) * P * TOPK,
                                 channel_multiplier=TOPK, allow_small_or_imprecise_dtypes=True))
                    lk(pool.memset(tbase[L][:], float((L - LANES) * P - 1)))
                table = route["table"][0:SLOTS, :].rearrange("(e c) o -> e (c o)", c=CAP)
                half = E // LANES
                for L in range(LANES):
                    rows = slice(L * half, (L + 1) * half)
                    pool.dma_start(table[rows, :], zero_row[rows, :]).then_inc(s_sct[L], 16)
                for L in range(LANES):
                    pool.wait_ge(s_sct[L], 16)
            pool.wait_ge(s_vec, 16 * nvec)
            if cross:
                chain.link(pool.tensor_scalar(rs[:], rs[:], 0.0, RES_MAX, ALU.max, ALU.min))
                chain.link(pool.tensor_tensor(rs2[:], rs[:], rs[:], ALU.mult))
            pool.memset(ready_mark[:], 0.0).then_inc(s_const, 1)

            def inv_std(L, s_ready, i, s_done, scaled=False):
                pool.wait_ge(s_ready[L], i + 1)
                dst = fac[L] if scaled else rstd[L]
                if scaled:
                    chain.link(pool.tensor_tensor(dst[:], mv[L][:, 1:2], rs2[:], ALU.mult))
                    chain.link(pool.tensor_tensor(dst[:], dst[:], eps[:], ALU.add))
                    chain.link(pool.tensor_tensor(dst[:], dst[:], minus_half[:], ALU.pow))
                    pool.tensor_tensor(dst[:], dst[:], rs[:], ALU.mult).then_inc(s_done[L], 1)
                else:
                    chain.link(pool.tensor_tensor(dst[:], mv[L][:, 1:2], eps[:], ALU.add))
                    pool.tensor_tensor(dst[:], dst[:], minus_half[:], ALU.pow).then_inc(s_done[L], 1)

            def residual(i, L, first):
                pool.wait_ge(s_x[L], 16 * (i + 1))
                if not first:
                    pool.wait_ge(s_x1[L], i)
                pool.tensor_tensor(xb[L][:], x_sb[L][:], (beta if cross else bias_out)[:], ALU.add).then_inc(s_xb[L], 1)

            def split_ctx(i, L, first):
                pool.wait_ge(s_ch[L], i + 1)
                if not first:
                    pool.wait_ge(s_m1[L], 3 * i)
                pool.tensor_tensor(cT[L][1][:], ctx_sb[L][:], cT[L][0][:].bitcast(F32), ALU.subtract).then_inc(s_cl[L], 1)

            def scatter(i, L):
                pool.wait_ge(s_ws[L], i + 1)
                if not isinstance(i, int):
                    pool.tensor_tensor(scratch_p[:, L:L + 1], eps[:], eps[:], ALU.mult)
                for k in range(TOPK):
                    pool.indirect_dma_start(out=route["table"], in_=token[L][:], in_offset=None,
                                            out_offset=bass.IndirectOffsetOnAxis(ap=wslot[L][:, k:k + 1], axis=0)
                                            ).then_inc(s_sct[L], 16)

            for L in range(LANES):
                inv_std(L, s_var, 0, s_rstd)
            before = chain.n
            per = LANES * (1 + (3 + 1 if cross else 0))
            chain.per = per

            def turn(i, first, last):
                chain.turn(i, before)
                for L in range(LANES):
                    if cross:
                        split_ctx(i, L, first)
                    residual(i, L, first)
                if not last:
                    for L in range(LANES):
                        inv_std(L, s_var, i + 1, s_rstd)
                if cross:
                    for L in range(LANES):
                        inv_std(L, s_var2, i, s_fac, scaled=True)
                    for L in range(LANES):
                        inv_std(L, s_var3, i, s_rstd3)
                if cross and not first:
                    for L in range(LANES):
                        scatter(i - 1, L)

            turn(0, True, False)
            with pool.Fori(1, PAIRS - 1) as i:
                turn(i, False, False)
            turn(PAIRS - 1, False, True)
            if cross:
                for L in range(LANES):
                    scatter(PAIRS - 1, L)

        @block.scalar
        def _(act):
            for n, (_, dst, m) in enumerate(pieces):
                act.wait_ge(s_stage[n % 2], 16 * (n // 2 + 1))
                act.activation(dst[0], stage[:, n % 2, 0:m], ACT.Copy).then_inc(s_hi, 1)

            def split_hi(bank, dst, s_in, i, s_done, L):
                act.wait_ge(s_in[L], i + 1)
                act.activation(dst[L][0][:], ps[L][:, bank, :], ACT.Copy).then_inc(s_done[L], 1)

            def turn(i, first):
                for L in range(LANES):
                    if cross:
                        act.wait_ge(s_c[L], 16 * (i + 1))
                        if not first:
                            act.wait_ge(s_m1[L], 3 * i)
                        act.activation(cT[L][0][:], ctx_sb[L][:], ACT.Copy).then_inc(s_ch[L], 1)
                    split_hi(3, xnT, s_t1, i, s_t1h, L)
                if cross and not first:
                    for L in range(LANES):
                        route_hi(i - 1, L)
                for L in range(LANES):
                    act.wait_ge(s_t2[L], 2 * i + 2)
                    for j in range(2):
                        r = slice(j * HD, (j + 1) * HD)
                        ins = act.activation(kbd[L][r, :, j, :], ps[L][r, 0, :].rearrange("p (c s) -> p c s", c=KC), ACT.Copy)
                    ins.then_inc(s_kbd[L], 1)
                    act.activation(qT[L][:], ps[L][:, 3, :], ACT.Copy).then_inc(s_qT[L], 1)
                if cross and not first:
                    for L in range(LANES):
                        route_exp(i - 1, L)
                for c in range(KC):
                    for L in range(LANES):
                        act.wait_ge(s_max[L], KC * i + c + 1)
                        heads = slice(c * HPC, (c + 1) * HPC)
                        if cross:
                            ins = act.activation(prb[L][:, heads, :], prb[L][:, heads, :], ACT.Exp, scale=SCALE)
                        else:
                            for h in range(c * HPC, (c + 1) * HPC):
                                ins = act.activation(prb[L][:, h, :], prb[L][:, h, :], ACT.Exp, bias=nmax[L][:, h:h + 1])
                        ins.then_inc(s_exp[L], 1)
                for c in range(KC):
                    for L in range(LANES):
                        act.wait_ge(s_pT[L], KC * i + c + 1)
                        act.activation(prb[L][:, c * HPC:(c + 1) * HPC, :],
                                       ps[L][:, c, :].rearrange("p (h s) -> p h s", h=HPC), ACT.Copy).then_inc(s_pTs[L], 1)
                for L in range(LANES):
                    split_hi(2, aT, s_t4, i, s_t4h, L)

            def route_hi(i, L):
                split_hi(3, xfT, s_t5, i, s_t5h, L)

            def route_exp(i, L):
                act.wait_ge(s_lm[L], i + 1)
                act.activation(prob[L][:], ps[L][:, 1, 0:E], ACT.Exp, bias=lneg[L][:], accum_out=lsum[L][:]).then_inc(s_le[L], 1)

            turn(0, True)
            with act.Fori(1, PAIRS) as i:
                turn(i, False)
            if cross:
                for L in range(LANES):
                    route_hi(PAIRS - 1, L)
                for L in range(LANES):
                    route_exp(PAIRS - 1, L)

        @block.vector
        def _(dve):
            chain = Chain(dve, s_dve)
            link = chain.link
            for n, (_, dst, m) in enumerate(pieces):
                dve.wait_ge(s_hi, n + 1)
                dve.tensor_tensor(dst[1], stage[:, n % 2, 0:m], dst[0].bitcast(F32), ALU.subtract).then_inc(s_lo, 1)
            dve.wait_ge(s_const, 1)
            if cross:
                for n in range(T // IM):
                    dve.wait_ge(s_mask, 16 * (n + 1))
                    part = nmask[:, n * IM:(n + 1) * IM]
                    link(dve.tensor_scalar(part, imask, 0.5, 1.0, ALU.is_gt, ALU.subtract))
                    dve.tensor_scalar(part, part, 1e30, None, ALU.mult).then_inc(s_nm, 1)
                    dve.wait_ge(s_nm, n + 1)

            def step_aside():
                dve.memset(scratch[:], 0.0)

            def norm_stats(src, L, s_done):
                link(dve.bn_stats(stats[L][:], src))
                step_aside()
                dve.bn_aggr(mv[L][:], stats[L][:]).then_inc(s_done[L], 1)

            def layernorm(i, L):
                dve.wait_ge(s_x[L], 16 * (i + 1))
                norm_stats(x_sb[L][:], L, s_var)

            def normed(i, L):
                dve.wait_ge(s_rstd[L], i + 1)
                dve.tensor_scalar(xn[L][:], x_sb[L][:], mv[L][:, 0:1], rstd[L][:, 0:1], ALU.subtract,
                                  ALU.mult).then_inc(s_xn[L], 1)

            def split_lo(bank, dst, s_hi_ready, i, s_done, L):
                dve.wait_ge(s_hi_ready[L], i + 1)
                dve.tensor_tensor(dst[L][1][:], ps[L][:, bank, :], dst[L][0][:].bitcast(F32), ALU.subtract).then_inc(s_done[L], 1)

            def qkv(i, L):
                for n, dst in enumerate((q_sb[L][:], k_sb[L][:], v_sb[L][:, :, 0:HD])):
                    dve.wait_ge(s_m1[L], 3 * i + n + 1)
                    src, b = ps[L][:, n, :], bias_in[:, n * H:(n + 1) * H]
                    if n == 2:
                        src, b = src.rearrange("p (h d) -> p h d", d=HD), b.rearrange("p (h d) -> p h d", d=HD)
                    dve.tensor_tensor(dst, src, b, ALU.add).then_inc((s_qk if n < 2 else s_v)[L], 1)

            def kT(i, L):
                dve.wait_ge(s_t2[L], 2 * i + 2)
                for j in range(2, HPC):
                    r = slice(j * HD, (j + 1) * HD)
                    ins = dve.tensor_copy(kbd[L][r, :, j, :], ps[L][r, 0, :].rearrange("p (c s) -> p c s", c=KC))
                ins.then_inc(s_kbd[L], 1)

            def mask(i, c, L):
                dve.wait_ge(s_sc[L], KC * i + c + 1)
                heads = slice(c * HPC, (c + 1) * HPC)
                out = prb[L][:, heads, :]
                src = ps[L][:, c, :].rearrange("p (h s) -> p h s", h=HPC)
                if cross:
                    m = nmask[:, bass.ds((i * LANES + L) * SEQ, SEQ)].unsqueeze(1).broadcast_to([P, HPC, SEQ])
                    link(dve.tensor_tensor(out, src, m, ALU.add))
                    dve.tensor_scalar(out, out, -CLIP / SCALE, CLIP / SCALE, ALU.max, ALU.min).then_inc(s_max[L], 1)
                else:
                    link(dve.tensor_tensor(out, src, tri_scale[:].unsqueeze(1).broadcast_to([P, HPC, SEQ]), ALU.mult))
                    link(dve.tensor_tensor(out, out, tri_neg[:].unsqueeze(1).broadcast_to([P, HPC, SEQ]), ALU.add))
                    dve.tensor_reduce(nmax[L][:, heads], out, AX, ALU.max, negate=True).then_inc(s_max[L], 1)

            def attention_out(i, L):
                dve.wait_ge(s_pv[L], i + 1)
                both = ps[L][:, 0:2, 0:NH // 2 * (HD + 1)].rearrange("p b (h d) -> p b h d", d=HD + 1)
                total = both[:, :, :, HD]
                r = rsum[L][:].rearrange("p (b h) -> p b h", b=2)
                link(dve.reciprocal(r, total))
                if cross:
                    r2 = rsum2[L][:].rearrange("p (b h) -> p b h", b=2)
                    link(dve.tensor_tensor(r2, total, r, ALU.mult))
                    link(dve.tensor_scalar(r2, r2, 1e-8, None, ALU.add))
                    link(dve.reciprocal(r2, r2))
                    link(dve.tensor_tensor(r, r, r2, ALU.mult))
                dve.tensor_tensor(attn[L][:].rearrange("p (b h d) -> p b h d", b=2, d=HD), both[:, :, :, 0:HD],
                                  r.unsqueeze(3).broadcast_to([P, 2, NH // 2, HD]), ALU.mult).then_inc(s_at[L], 1)

            def output(i, L, first):
                dve.wait_ge(s_o[L], i + 1)
                dve.wait_ge(s_xb[L], i + 1)
                if not first:
                    dve.wait_ge(s_st[L], 16 * i)
                if not cross:
                    dve.tensor_tensor(x1[L][:], ps[L][:, 3, :], xb[L][:], ALU.add).then_inc(s_x1[L], 1)
                else:
                    dve.tensor_tensor(dlt[L][:], ps[L][:, 3, :], bias_out[:], ALU.add).then_inc(s_of[L], 1)
                    dve.wait_ge(s_of[L], i + 1)
                    norm_stats(dlt[L][:], L, s_var2)

            def delta(i, L):
                dve.wait_ge(s_fac[L], i + 1)
                link(dve.tensor_scalar(dlt[L][:], dlt[L][:], mv[L][:, 0:1], fac[L][:, 0:1], ALU.subtract, ALU.mult))
                link(dve.tensor_tensor(dlt[L][:], dlt[L][:], gamma[:], ALU.mult))
                dve.tensor_tensor(x1[L][:], dlt[L][:], xb[L][:], ALU.add).then_inc(s_x1[L], 1)
                dve.wait_ge(s_x1[L], i + 1)
                norm_stats(x1[L][:], L, s_var3)

            def final_norm(i, L, first):
                dve.wait_ge(s_rstd3[L], i + 1)
                if not first:
                    dve.wait_ge(s_stf[L], 16 * i)
                    dve.wait_ge(s_t5[L], i)
                dve.tensor_scalar(xf[L][:], x1[L][:], mv[L][:, 0:1], rstd[L][:, 0:1], ALU.subtract,
                                  ALU.mult).then_inc(s_xf[L], 1)

            def route_max(i, L):
                dve.wait_ge(s_lg[L], i + 1)
                dve.tensor_reduce(lneg[L][:], ps[L][:, 1, 0:E], AX, ALU.max, negate=True).then_inc(s_lm[L], 1)

            def route_choose(i, L):
                b = i * LANES + L
                dve.wait_ge(s_le[L], i + 1)
                link(dve.reciprocal(lsum[L][:], lsum[L][:]))
                link(dve.tensor_scalar(prob[L][:], prob[L][:], lsum[L][:, 0:1], None, ALU.mult))
                grouped = prob[L][:].rearrange("p (g n) -> p g n", g=GROUPS)
                link(dve.tensor_reduce(gmax[L][:], grouped, AX, ALU.max))
                step_aside()
                link(dve.max(gtop[L][:], gmax[L][:]))
                step_aside()
                link(dve.max_index(gidx[L][:], gtop[L][:], gmax[L][:]))
                link(dve.tensor_copy(gidf[L][:], gidx[L][:]))
                link(dve.tensor_tensor(gone[L][:], iota8[:].unsqueeze(1).broadcast_to([P, TOPG, GROUPS]),
                                       gidf[L][:, 0:TOPG].unsqueeze(2).broadcast_to([P, TOPG, GROUPS]), ALU.is_equal))
                link(dve.tensor_reduce(gmask[L][:], gone[L][:].rearrange("p k g -> p g k"), AX, ALU.add))
                link(dve.tensor_tensor(grouped, grouped, gmask[L][:].unsqueeze(2).broadcast_to([P, GROUPS, GSIZE]), ALU.mult))
                step_aside()
                link(dve.max(top[L][:], prob[L][:]))
                step_aside()
                link(dve.max_index(tidx[L][:], top[L][:], prob[L][:]))
                link(dve.tensor_copy(tidf[L][:], tidx[L][:]))
                dve.tensor_copy(route["weight"][:, bass.ds(b * TOPK, TOPK)], top[L][:, 0:TOPK])
                link(dve.tensor_tensor(onehot[L][:], iota64[:].unsqueeze(1).broadcast_to([P, TOPK, E]),
                                       tidf[L][:, 0:TOPK].unsqueeze(2).broadcast_to([P, TOPK, E]), ALU.is_equal))
                with nc.allow_low_precision(reason="zeros and a single one are summed"):
                    dve.tensor_reduce(chosen[L][:], onehot[L][:].rearrange("p k e -> p e k"), AX, ALU.add).then_inc(s_choice[L], 1)

            def route_positions(i, L):
                dve.wait_ge(s_pos[L], i + 1)
                link(dve.tensor_tensor(posn[L][:], ps[L][:, 3, 0:E], count[:], ALU.add))
                link(dve.tensor_tensor(count[:], count[:], ps[L][:, 3, E:2 * E], ALU.add))
                dve.tensor_reduce(lmax[L][:], ps[L][0:E, 3, P:2 * P], AX, ALU.max).then_inc(s_posd[L], 1)

            def route_slots(i, L):
                b = i * LANES + L
                dve.wait_ge(s_posd[L], i + 1)
                link(dve.tensor_scalar(tbase[L][:], tbase[L][:], float(LANES * P), None, ALU.add))
                link(dve.tensor_scalar(lpos[L][:], lmax[L][:], 0.0, None, ALU.is_gt))
                link(dve.tensor_tensor(lmax[L][:], lmax[L][:], tbase[L][:], ALU.add))
                link(dve.tensor_tensor(lmax[L][:], lmax[L][:], lpos[L][:], ALU.mult))
                link(dve.tensor_tensor(last_tok[:], last_tok[:], lmax[L][:], ALU.max))
                link(dve.tensor_tensor(onehot[L][:], onehot[L][:], posn[L][:].unsqueeze(1).broadcast_to([P, TOPK, E]), ALU.mult))
                link(dve.tensor_reduce(posk[L][:], onehot[L][:], AX, ALU.add))
                link(dve.tensor_scalar(over[L][:], posk[L][:], float(CAP - 1), None, ALU.is_ge))
                link(dve.tensor_scalar(posk[L][:], posk[L][:], float(CAP - 1), None, ALU.min))
                link(dve.scalar_tensor_tensor(slot[L][:], tidf[L][:, 0:TOPK], float(CAP), posk[L][:], ALU.mult, ALU.add))
                dve.tensor_copy(route["slot"][:, bass.ds(b * TOPK, TOPK)], slot[L][:])
                dve.wait_ge(s_sct[L], 16 * TOPK * i + 16)
                link(dve.tensor_scalar(dump[L][:], dump[L][:], float(LANES * P * TOPK), None, ALU.add))
                link(dve.tensor_tensor(posk[L][:], dump[L][:], slot[L][:], ALU.subtract))
                link(dve.tensor_tensor(posk[L][:], posk[L][:], over[L][:], ALU.mult))
                link(dve.tensor_scalar(token[L][:], token[L][:], float(LANES * P), None, ALU.add))
                dve.tensor_tensor(wslot[L][:], slot[L][:], posk[L][:], ALU.add).then_inc(s_ws[L], 1)

            R_CHOOSE, R_SLOTS = 13, 16
            for L in range(LANES):
                layernorm(0, L)
            for L in range(LANES):
                normed(0, L)
            before = chain.n
            if cross:
                chain.per = LANES * (KC + 5 + 1 + 1 + 2 + 1 + R_CHOOSE + R_SLOTS)
                skipped_first = LANES * (R_CHOOSE + R_SLOTS)
                before -= skipped_first
            else:
                chain.per = LANES * (2 * KC + 1 + 1)
                skipped_first = 0

            def turn(i, first, last):
                chain.turn(i, before)
                if first:
                    chain.base += skipped_first
                for L in range(LANES):
                    split_lo(3, xnT, s_t1h, i, s_t1l, L)
                for L in range(LANES):
                    qkv(i, L)
                if cross and not first:
                    for L in range(LANES):
                        split_lo(3, xfT, s_t5h, i - 1, s_t5l, L)
                for L in range(LANES):
                    kT(i, L)
                if cross and not first:
                    for L in range(LANES):
                        route_max(i - 1, L)
                for c in range(KC):
                    for L in range(LANES):
                        mask(i, c, L)
                if cross and not first:
                    for L in range(LANES):
                        route_choose(i - 1, L)
                if not last:
                    for L in range(LANES):
                        layernorm(i + 1, L)
                    for L in range(LANES):
                        normed(i + 1, L)
                for L in range(LANES):
                    attention_out(i, L)
                if cross and not first:
                    for L in range(LANES):
                        route_positions(i - 1, L)
                for L in range(LANES):
                    split_lo(2, aT, s_t4h, i, s_t4l, L)
                if cross and not first:
                    for L in range(LANES):
                        route_slots(i - 1, L)
                for L in range(LANES):
                    output(i, L, first)
                if cross:
                    for L in range(LANES):
                        delta(i, L)
                    for L in range(LANES):
                        final_norm(i, L, first)
                n = chain.n + (skipped_first if first else 0) + (LANES if last else 0)
                assert n == chain.per, (n, chain.per)

            turn(0, True, False)
            with dve.Fori(1, PAIRS - 1) as i:
                turn(i, False, False)
            turn(PAIRS - 1, False, True)
            if cross:
                i = PAIRS - 1
                for L in range(LANES):
                    split_lo(3, xfT, s_t5h, i, s_t5l, L)
                for L in range(LANES):
                    route_max(i, L)
                for L in range(LANES):
                    route_choose(i, L)
                for L in range(LANES):
                    route_positions(i, L)
                for L in range(LANES):
                    route_slots(i, L)
                dve.tensor_copy(last_tok[:], last_tok[:]).then_inc(s_last, 1)

        @block.tensor
        def _(pe):
            def project(bank, i, L, x, w, cols):
                for k in range(KC):
                    ks = slice(k * P, (k + 1) * P)
                    ins = matmul3(pe, ps[L][:, bank, 0:cols.stop - cols.start], (x[0][:, ks], x[1][:, ks]),
                                  (w[0][:, k, cols], w[1][:, k, cols]), k == 0, k == KC - 1)
                return ins

            def route_turn(i, L):
                pe.wait_ge(s_xf[L], i + 1)
                transpose4(pe, ps[L][:, 3, :], xf[L][:], ident[:]).then_inc(s_t5[L], 1)

            def route_logits(i, L):
                pe.wait_ge(s_t5l[L], i + 1)
                project(1, i, L, xfT[L], gate, slice(0, E)).then_inc(s_lg[L], 1)

            def route_count(i, L):
                pe.wait_ge(s_choice[L], i + 1)
                pe.matmul(ps[L][:, 3, 0:E], before_me[:], chosen[L][:], start=True, stop=True)
                pe.matmul(ps[L][:, 3, E:2 * E], all_ones[:], chosen[L][:], start=True, stop=True)
                pe.matmul(ps[L][0:E, 3, P:2 * P], chosen[L][:], diag_pos[:], start=True, stop=True).then_inc(s_pos[L], 1)

            def turn(i, first):
                for L in range(LANES):
                    pe.wait_ge(s_xn[L], i + 1)
                    if not first:
                        pe.wait_ge((s_of if cross else s_x1)[L], i)
                    transpose4(pe, ps[L][:, 3, :], xn[L][:], ident[:]).then_inc(s_t1[L], 1)
                for L in range(LANES):
                    if cross:
                        pe.wait_ge(s_cl[L], i + 1)
                    pe.wait_ge(s_t1l[L], i + 1)
                    kv = cT[L] if cross else xnT[L]
                    for n in range(3):
                        project(n, i, L, xnT[L] if n == 0 else kv, wi, slice(n * H, (n + 1) * H)).then_inc(s_m1[L], 1)
                if cross and not first:
                    for L in range(LANES):
                        route_turn(i - 1, L)
                for L in range(LANES):
                    pe.wait_ge(s_qk[L], 2 * i + 2)
                    if cross and not first:
                        pe.wait_ge(s_t5l[L], i)
                    transpose4(pe, ps[L][:, 3, :], q_sb[L][:], ident[:]).then_inc(s_t2[L], 1)
                    transpose4(pe, ps[L][:, 0, :], k_sb[L][:], ident[:]).then_inc(s_t2[L], 1)
                if cross and not first:
                    for L in range(LANES):
                        route_logits(i - 1, L)
                for c in range(KC):
                    for L in range(LANES):
                        if c == 0:
                            pe.wait_ge(s_kbd[L], 2 * i + 2)
                            pe.wait_ge(s_qT[L], i + 1)
                        if c == 1 and cross and not first:
                            pe.wait_ge(s_le[L], i)
                        if c == 2:
                            pe.wait_ge(s_v[L], i + 1)
                        pe.matmul(ps[L][:, c, :], qT[L][:, c * P:(c + 1) * P], kbd[L][:, c, :, :], start=True,
                                  stop=True).then_inc(s_sc[L], 1)
                for c in range(KC):
                    for L in range(LANES):
                        pe.wait_ge(s_exp[L], KC * i + c + 1)
                        for j in range(HPC):
                            ins = pe.transpose(ps[L][:, c, j * P:(j + 1) * P], prb[L][:, c * HPC + j, :], ident[:])
                        ins.then_inc(s_pT[L], 1)
                for c in range(KC):
                    for L in range(LANES):
                        pe.wait_ge(s_pTs[L], KC * i + max(c + 1, 2))
                        for h in range(c * HPC, (c + 1) * HPC):
                            at = h % (NH // 2) * (HD + 1)
                            ins = pe.matmul(ps[L][:, h // (NH // 2), at:at + HD + 1], prb[L][:, h, :], v_sb[L][:, h, :],
                                            start=True, stop=True)
                        if c == KC - 1:
                            ins.then_inc(s_pv[L], 1)
                if cross and not first:
                    for L in range(LANES):
                        route_count(i - 1, L)
                for L in range(LANES):
                    pe.wait_ge(s_at[L], i + 1)
                    transpose4(pe, ps[L][:, 2, :], attn[L][:], ident[:]).then_inc(s_t4[L], 1)
                for L in range(LANES):
                    pe.wait_ge(s_t4l[L], i + 1)
                    if cross and not first:
                        pe.wait_ge(s_posd[L], i)
                    project(3, i, L, aT[L], wo, slice(0, H)).then_inc(s_o[L], 1)

            pe.wait_ge(s_lo, len(pieces))
            pe.wait_ge(s_const, 1)
            turn(0, True)
            with pe.Fori(1, PAIRS) as i:
                turn(i, False)
            if cross:
                i = PAIRS - 1
                for L in range(LANES):
                    route_turn(i, L)
                for L in range(LANES):
                    route_logits(i, L)
                for L in range(LANES):
                    route_count(i, L)


M, MCH = 352, ((0, 128), (128, 128), (256, 96))
HALF = CAP // 2
COLS = LANES * CAP // P
MS = 704
SCH = ((0, 128), (128, 128), (256, 128), (384, 128), (512, 96), (608, 96))
QT = 4


def expert_phase(nc, wg_in, wu_in, wd_in, xf, table, y_out, ident):
    turns = E // 2
    with ExitStack() as ctx:
        def sb(name, shape, dt=F32):
            return ctx.enter_context(nc.sbuf_tensor("e_" + name, shape, dt))

        def pb(name):
            return ctx.enter_context(nc.psum_tensor("e_" + name, [P, 512], F32))

        sems = []

        def sem(name):
            sems.append(nc.alloc_semaphore("e_" + name))
            return sems[-1]

        def two(make, name, *a):
            return [make(f"{name}{b}", *a) for b in range(2)]

        names_row = sb("names_row", [E * CAP // P, P])
        names = sb("names", [P, E * CAP // P], U32)
        idx = sb("idx", [P, COLS], U32)
        carry = sb("carry", [P, 1])
        xones = sb("ones", [P, 1])
        xg = sb("xg", [P, COLS * H])
        xT = [sb("xT_hi", [P, KC, COLS * P], F32R), sb("xT_lo", [P, KC, COLS * P], F32R)]
        raw_g, raw_u = two(sb, "raw_g", [P, KC, M]), two(sb, "raw_u", [P, KC, M])
        raw_d = two(sb, "raw_d", [P, 3, H])
        wg, wu = ([two(sb, f"{n}_{b}", [P, KC, M], F32R) for b in range(2)] for n in ("wg", "wu"))
        wd = [two(sb, f"wd_{b}", [P, 3, H], F32R) for b in range(2)]
        act_g = two(sb, "act_g", [P, 3, CAP])
        h_raw = two(sb, "h_raw", [P, 3, CAP])
        hid = [two(sb, f"hid_{b}", [P, 3, CAP], F32R) for b in range(2)]
        y_sb = two(sb, "y", [HALF, 2, H])
        gu = [pb(f"gu{m}") for m in range(3)]
        dn = [pb(f"dn{h}") for h in range(2)]
        tr = [pb(f"tr{j}") for j in range(COLS)]

        s_row = sem("names_loaded")
        s_ones = sem("ones_ready")
        s_nT = sem("names_in_psum")
        s_names = sem("names_ready")
        s_idx = sem("idx_ready")
        s_x = [sem(f"tokens_gathered{j}") for j in range(COLS)]
        s_lg, s_lu, s_ld = two(sem, "wg_loaded"), two(sem, "wu_loaded"), two(sem, "wd_loaded")
        s_guh, s_gul = two(sem, "wgu_hi_ready"), two(sem, "wgu_lo_ready")
        s_dh, s_dl = two(sem, "wd_hi_ready"), two(sem, "wd_lo_ready")
        s_t = sem("xT_in_psum")
        s_th = sem("xT_hi_ready")
        s_tl = sem("xT_lo_ready")
        s_gu = sem("gate_up_in_psum")
        s_silu = sem("silu_ready")
        s_mul = sem("hidden_ready")
        s_hh = sem("hidden_hi_ready")
        s_hl = sem("hidden_lo_ready")
        s_dn = sem("down_in_psum")
        s_y = [sem("y_half0_ready"), sem("y_half1_ready")]
        s_st = two(sem, "y_stored")

        ctx.callback(end_phase, nc, sems)
        block = ctx.enter_context(nc.Block())

        def nxt(g, b):
            return (g, 1) if b == 0 else (g + 1, 0)

        def before(g, b, n):
            if isinstance(g, int) and 2 * g + b < n:
                return None
            if n == 1:
                return (g, 0) if b == 1 else (g - 1, 1)
            return (g - 1, b)

        @block.sync
        def _(sp):
            def load_gu(g, b, first):
                if not first:
                    sp.wait_ge(s_gul[b], 2 * g)
                rows = bass.ds((2 * g + b) * P, P)
                sp.dma_start(raw_g[b][:].rearrange("p k m -> p (k m)"), wg_in[rows, :]).then_inc(s_lg[b], 16)
                sp.dma_start(raw_u[b][:].rearrange("p k m -> p (k m)"), wu_in[rows, :]).then_inc(s_lu[b], 16)

            def load_d(g, b, first):
                if not first:
                    sp.wait_ge(s_dl[b], 2 * g)
                row = (2 * g + b) * M
                sp.dma_start(raw_d[b][:, 0:2, :], wd_in[bass.ds(row, 2 * P), :].rearrange("(c p) n -> p c n", p=P)
                             ).then_inc(s_ld[b], 16)
                sp.dma_start(raw_d[b][0:96, 2, :], wd_in[bass.ds(row + 2 * P, 96), :]).then_inc(s_ld[b], 16)

            def store(g, b):
                e = 2 * g + b
                sp.wait_ge(s_y[0], e + 1)
                sp.wait_ge(s_y[1], e + 1)
                sp.dma_start(y_out[bass.ds(e * CAP, CAP), :].rearrange("(f p) n -> p f n", p=HALF), y_sb[b][:]
                             ).then_inc(s_st[b], 16)

            sp.dma_start(names_row[:], table[0:SLOTS, :].rearrange("(c p) o -> c (p o)", p=P)).then_inc(s_row, 16)
            for b in range(2):
                load_gu(0, b, True)
                load_d(0, b, True)
            load_gu(1, 0, False)

            def turn(g, first, last):
                if not last:
                    if not first:
                        load_gu(g + 1, 0, False)
                    load_gu(g + 1, 1, False)
                    load_d(g + 1, 0, False)
                if not first:
                    store(g - 1, 0)
                    store(g - 1, 1)
                if not last:
                    load_d(g + 1, 1, False)

            turn(0, True, False)
            with sp.Fori(1, turns - 1) as g:
                turn(g, False, False)
            turn(turns - 1, False, True)
            for b in range(2):
                store(turns - 1, b)
            for b in range(2):
                sp.wait_ge(s_st[b], 16 * turns)

        @block.gpsimd
        def _(pool):
            def gather(g, first):
                if not first:
                    pool.wait_ge(s_t, COLS * g)
                pool.tensor_copy(idx[:], names[:, bass.ds(g * COLS, COLS)]).then_inc(s_idx, 1)
                pool.wait_ge(s_idx, g + 1)
                if not isinstance(g, int):
                    pool.tensor_tensor(carry[:], xones[:], xones[:], ALU.mult)
                for j in range(COLS):
                    pool.indirect_dma_start(out=xg[:, j * H:(j + 1) * H], out_offset=None, in_=xf,
                                            in_offset=bass.IndirectOffsetOnAxis(ap=idx[:, j:j + 1], axis=0)
                                            ).then_inc(s_x[j], 16)

            def hidden_lo(g, b):
                for c, (_, n) in enumerate(MCH):
                    e = 2 * g + b
                    pool.wait_ge(s_hh, 3 * e + c + 1)
                    f = before(g, b, 2)
                    if f is not None:
                        pool.wait_ge(s_dn, 2 * (2 * f[0] + b) + 2)
                    pool.tensor_tensor(hid[b][1][0:n, c, :], h_raw[b][0:n, c, :], hid[b][0][0:n, c, :].bitcast(F32),
                                       ALU.subtract).then_inc(s_hl, 1)

            pool.memset(xones[:], 1.0).then_inc(s_ones, 1)
            pool.wait_ge(s_ones, 1)
            pool.wait_ge(s_names, 1)
            gather(0, True)

            def turn(g, last):
                if not last:
                    gather(g + 1, False)
                for b in range(2):
                    hidden_lo(g, b)

            turn(0, False)
            with pool.Fori(1, turns - 1) as g:
                turn(g, False)
            turn(turns - 1, True)

        @block.scalar
        def _(act):
            def gu_hi(g, b, which):
                raw, w, s = ((raw_g, wg, s_lg), (raw_u, wu, s_lu))[which]
                act.wait_ge(s[b], 16 * (g + 1))
                f = before(g, b, 2)
                if f is not None:
                    act.wait_ge(s_mul, 3 * (2 * f[0] + b) + 3)
                act.activation(w[b][0][:], raw[b][:], ACT.Copy).then_inc(s_guh[b], 1)

            def d_hi(g, b, part):
                if part == 0:
                    act.wait_ge(s_ld[b], 32 * (g + 1))
                f = before(g, b, 2)
                if f is not None:
                    act.wait_ge(s_dn, 2 * (2 * f[0] + b) + 2)
                rows, cs = ((P, slice(0, 2)), (96, slice(2, 3)))[part]
                act.activation(wd[b][0][0:rows, cs, :], raw_d[b][0:rows, cs, :], ACT.Copy).then_inc(s_dh[b], 1)

            def silu(g, b, c):
                n = MCH[c][1]
                act.wait_ge(s_gu, 3 * (2 * g + b) + c + 1)
                act.activation(act_g[b][0:n, c, :], gu[c][0:n, 0:CAP], ACT.Silu).then_inc(s_silu, 1)

            def hidden_hi(g, b, c):
                n = MCH[c][1]
                act.wait_ge(s_mul, 3 * (2 * g + b) + c + 1)
                act.activation(hid[b][0][0:n, c, :], h_raw[b][0:n, c, :], ACT.Copy).then_inc(s_hh, 1)

            def x_hi(g):
                for j in range(COLS):
                    act.wait_ge(s_t, COLS * g + j + 1)
                    act.activation(xT[0][:, :, j * P:(j + 1) * P], tr[j][:].rearrange("p (k s) -> p k s", k=KC),
                                   ACT.Copy).then_inc(s_th, 1)

            def y_half(g, b):
                act.wait_ge(s_dn, 2 * (2 * g + b) + 1)
                if not (isinstance(g, int) and g == 0):
                    act.wait_ge(s_st[b], 16 * g)
                act.activation(y_sb[b][:, 0, :], dn[0][0:HALF, :], ACT.Copy).then_inc(s_y[0], 1)

            def half(g, b, last):
                f = before(g, b, 2)
                if f is not None:
                    y_half(*f)
                more = not (last and b == 1)
                if more:
                    gu_hi(*nxt(g, b), 0)
                silu(g, b, 0)
                if more:
                    gu_hi(*nxt(g, b), 1)
                hidden_hi(g, b, 0)
                silu(g, b, 1)
                d_hi(g, b, 0)
                hidden_hi(g, b, 1)
                silu(g, b, 2)
                d_hi(g, b, 1)
                hidden_hi(g, b, 2)
                if b == 1 and not last:
                    x_hi(g + 1)

            gu_hi(0, 0, 0)
            gu_hi(0, 0, 1)
            x_hi(0)
            for b in range(2):
                half(0, b, False)
            with act.Fori(1, turns - 1) as g:
                for b in range(2):
                    half(g, b, False)
            for b in range(2):
                half(turns - 1, b, True)
            for b in range(2):
                y_half(turns - 1, b)

        @block.vector
        def _(dve):
            def gu_lo(g, b, which):
                raw, w = ((raw_g, wg), (raw_u, wu))[which]
                dve.wait_ge(s_guh[b], 2 * g + which + 1)
                dve.tensor_tensor(w[b][1][:], raw[b][:], w[b][0][:].bitcast(F32), ALU.subtract).then_inc(s_gul[b], 1)

            def d_lo(g, b, part):
                dve.wait_ge(s_dh[b], 2 * g + part + 1)
                rows, cs = ((P, slice(0, 2)), (96, slice(2, 3)))[part]
                dve.tensor_tensor(wd[b][1][0:rows, cs, :], raw_d[b][0:rows, cs, :], wd[b][0][0:rows, cs, :].bitcast(F32),
                                  ALU.subtract).then_inc(s_dl[b], 1)

            def hidden(g, b, c):
                n, e = MCH[c][1], 2 * g + b
                dve.wait_ge(s_silu, 3 * e + c + 1)
                f = before(g, b, 2)
                if f is not None:
                    dve.wait_ge(s_hl, 3 * (2 * f[0] + b) + c + 1)
                dve.tensor_tensor(h_raw[b][0:n, c, :], gu[c][0:n, CAP:2 * CAP], act_g[b][0:n, c, :], ALU.mult).then_inc(s_mul, 1)

            def x_lo(g):
                for j in range(COLS):
                    dve.wait_ge(s_th, COLS * g + j + 1)
                    cols = slice(j * P, (j + 1) * P)
                    dve.tensor_tensor(xT[1][:, :, cols], tr[j][:].rearrange("p (k s) -> p k s", k=KC),
                                      xT[0][:, :, cols].bitcast(F32), ALU.subtract).then_inc(s_tl, 1)

            def y_half(g, b):
                dve.wait_ge(s_dn, 2 * (2 * g + b) + 2)
                if not (isinstance(g, int) and g == 0):
                    dve.wait_ge(s_st[b], 16 * g)
                dve.tensor_copy(y_sb[b][:, 1, :], dn[1][0:HALF, :]).then_inc(s_y[1], 1)

            def half(g, b, last):
                f = before(g, b, 2)
                if f is not None:
                    y_half(*f)
                more = not (last and b == 1)
                if more:
                    gu_lo(*nxt(g, b), 0)
                hidden(g, b, 0)
                if more:
                    gu_lo(*nxt(g, b), 1)
                hidden(g, b, 1)
                d_lo(g, b, 0)
                hidden(g, b, 2)
                d_lo(g, b, 1)
                if b == 1 and not last:
                    x_lo(g + 1)

            dve.wait_ge(s_nT, 1)
            dve.tensor_copy(names[:], gu[0][:, 0:E * CAP // P]).then_inc(s_names, 1)
            gu_lo(0, 0, 0)
            gu_lo(0, 0, 1)
            x_lo(0)
            for b in range(2):
                half(0, b, False)
            with dve.Fori(1, turns - 1) as g:
                for b in range(2):
                    half(g, b, False)
            for b in range(2):
                half(turns - 1, b, True)
            for b in range(2):
                y_half(turns - 1, b)

        @block.tensor
        def _(pe):
            def turn_tokens(g):
                for j in range(COLS):
                    pe.wait_ge(s_x[j], 16 * (g + 1))
                    transpose4(pe, tr[j], xg[:, j * H:(j + 1) * H], ident[:]).then_inc(s_t, 1)

            def gate_up(g, b):
                e = 2 * g + b
                if b == 0:
                    pe.wait_ge(s_tl, COLS * (g + 1))
                pe.wait_ge(s_gul[b], 2 * (g + 1))
                toks = slice(b * CAP, (b + 1) * CAP)
                for c, (m, n) in enumerate(MCH):
                    f = before(g, b, 1)
                    if f is not None:
                        pe.wait_ge(s_mul, 3 * (2 * f[0] + f[1]) + c + 1)
                    for w, at in ((wg, 0), (wu, CAP)):
                        for k in range(KC):
                            ins = matmul3(pe, gu[c][0:n, at:at + CAP], (w[b][0][:, k, m:m + n], w[b][1][:, k, m:m + n]),
                                          (xT[0][:, k, toks], xT[1][:, k, toks]), k == 0, k == KC - 1)
                    ins.then_inc(s_gu, 1)

            def down(g, b):
                e = 2 * g + b
                pe.wait_ge(s_dl[b], 2 * (g + 1))
                pe.wait_ge(s_hl, 3 * e + 3)
                f = before(g, b, 1)
                for hf in range(2):
                    if f is not None:
                        pe.wait_ge(s_y[hf], 2 * f[0] + f[1] + 1)
                    toks = slice(hf * HALF, (hf + 1) * HALF)
                    for c, (_, n) in enumerate(MCH):
                        ins = matmul3(pe, dn[hf][0:HALF, :], (hid[b][0][0:n, c, toks], hid[b][1][0:n, c, toks]),
                                      (wd[b][0][0:n, c, :], wd[b][1][0:n, c, :]), c == 0, c == 2)
                    ins.then_inc(s_dn, 1)

            pe.wait_ge(s_row, 16)
            pe.transpose(gu[0][:, 0:E * CAP // P], names_row[:], ident[0:E * CAP // P, 0:E * CAP // P]).then_inc(s_nT, 1)
            turn_tokens(0)
            pe.wait_ge(s_names, 1)

            def turn(g, last):
                gate_up(g, 0)
                f = before(g, 0, 1)
                if f is not None:
                    down(*f)
                gate_up(g, 1)
                if not last:
                    turn_tokens(g + 1)
                down(g, 0)

            turn(0, False)
            with pe.Fori(1, turns - 1) as g:
                turn(g, False)
            turn(turns - 1, True)
            down(turns - 1, 1)


def shared_phase(nc, sg_in, su_in, sd_in, xf, x3, y_in, out, weight, slot, ident):
    quads = BATCH // QT
    with ExitStack() as ctx:
        def sb(name, shape, dt=F32):
            return ctx.enter_context(nc.sbuf_tensor("h_" + name, shape, dt))

        def pb(name):
            return ctx.enter_context(nc.psum_tensor("h_" + name, [P, 512], F32))

        sems = []

        def sem(name):
            sems.append(nc.alloc_semaphore("h_" + name))
            return sems[-1]

        def two(make, name, *a):
            return [make(f"{name}{b}", *a) for b in range(2)]

        sg, su = two(sb, "sg_", [P, KC, MS], F32R), two(sb, "su_", [P, KC, MS], F32R)
        sd = two(sb, "sd_", [P, len(SCH), H], F32R)
        stage = sb("stage", [P, 2, MS])
        xf_sb = sb("xf", [P, QT, H])
        xT = two(sb, "xT_", [P, KC, QT * P], F32R)
        act_g = two(sb, "act_g", [P, QT * P])
        h_raw = two(sb, "h_raw", [P, QT * P])
        hid = two(sb, "hid_", [P, len(SCH), QT * P], F32R)
        yk = two(sb, "yk", [P, TOPK * H])
        acc = two(sb, "acc", [P, H])
        o_sb = two(sb, "o", [P, H])
        idx = two(sb, "idx", [P, TOPK], U32)
        w_t = two(sb, "w_t", [P, TOPK])
        carry = two(sb, "carry", [P, 1])
        ones = sb("ones", [P, 1])
        tr, gt, up, dn = two(pb, "tr"), two(pb, "gt"), two(pb, "up"), two(pb, "dn")

        s_stage = two(sem, "stage_loaded")
        s_wh, s_wl = sem("weight_hi"), sem("weight_lo")
        s_xf = sem("xf_loaded")
        s_t, s_th, s_tl = sem("xT_in_psum"), sem("xT_hi_ready"), sem("xT_lo_ready")
        s_gu, s_silu, s_mul = sem("gate_up_in_psum"), sem("silu_ready"), sem("hidden_ready")
        s_hh, s_hl = sem("hidden_hi_ready"), sem("hidden_lo_ready")
        s_dn = sem("down_in_psum")
        s_x3 = two(sem, "x3_loaded")
        s_idx = two(sem, "idx_ready")
        s_yk = [[sem(f"rows_gathered{b}_{k}") for k in range(TOPK)] for b in range(2)]
        s_wt = two(sem, "weights_ready")
        s_acc = two(sem, "routed_sum_step")
        s_o = two(sem, "out_ready")
        s_st = two(sem, "out_stored")
        s_ones = sem("ones_ready")

        pieces = []
        for k in range(KC):
            for src, w in ((sg_in, sg), (su_in, su)):
                pieces.append((src[k * P:(k + 1) * P, :], [d[:, k, :] for d in w], P, MS))
        for c, (m, n) in enumerate(SCH):
            pieces.append((sd_in[m:m + n, :], [d[0:n, c, :] for d in sd], n, H))

        ctx.callback(end_phase, nc, sems)
        block = ctx.enter_context(nc.Block())
        per_tile = 1 + TOPK

        @block.sync
        def _(sp):
            def load_xf(q):
                sp.dma_start(xf_sb[:], xf[bass.ds(q * QT * P, QT * P), :].rearrange("(t p) h -> p t h", p=P)).then_inc(s_xf, 16)

            def load_x3(q, t, first):
                b = t % 2
                if not first:
                    sp.wait_ge(s_o[b], q * (QT // 2) + t // 2)
                sp.dma_start(acc[b][:], x3[bass.ds((q * QT + t) * P, P), :]).then_inc(s_x3[b], 16)

            def store(q, t):
                b = t % 2
                sp.wait_ge(s_o[b], q * (QT // 2) + t // 2 + 1)
                sp.dma_start(out[bass.ds((q * QT + t) * P, P), :], o_sb[b][:]).then_inc(s_st[b], 16)

            load_xf(0)
            for t in range(2):
                load_x3(0, t, True)
            for n, (src, _, rows, cols) in enumerate(pieces):
                if n >= 2:
                    sp.wait_ge(s_wl, n - 1)
                sp.dma_start(stage[0:rows, n % 2, 0:cols], src).then_inc(s_stage[n % 2], 16)

            def turn(q, last):
                if not last:
                    sp.wait_ge(s_t, QT * (q + 1))
                    load_xf(q + 1)
                for t in range(QT):
                    store(q, t)
                    if not (last and t >= QT - 2):
                        nq, nt = (q, t + 2) if t + 2 < QT else (q + 1, t + 2 - QT)
                        load_x3(nq, nt, False)

            with sp.Fori(0, quads - 1) as q:
                turn(q, False)
            turn(quads - 1, True)
            for b in range(2):
                sp.wait_ge(s_st[b], 16 * BATCH // 2)

        @block.gpsimd
        def _(pool):
            pool.memset(ones[:], 1.0).then_inc(s_ones, 1)
            pool.wait_ge(s_ones, 1)

            def gather(q, t, first):
                b = t % 2
                n = q * (QT // 2) + t // 2
                if not first:
                    pool.wait_ge(s_acc[b], TOPK * n)
                pool.tensor_copy(idx[b][:], slot[:, bass.ds((q * QT + t) * TOPK, TOPK)]).then_inc(s_idx[b], 1)
                pool.wait_ge(s_idx[b], n + 1)
                if not isinstance(q, int):
                    pool.tensor_tensor(carry[b][:], ones[:], ones[:], ALU.mult)
                for k in range(TOPK):
                    pool.indirect_dma_start(out=yk[b][:, k * H:(k + 1) * H], out_offset=None, in_=y_in,
                                            in_offset=bass.IndirectOffsetOnAxis(ap=idx[b][:, k:k + 1], axis=0)
                                            ).then_inc(s_yk[b][k], 16)

            for t in range(QT):
                gather(0, t, t < 2)
            with pool.Fori(1, quads) as q:
                for t in range(QT):
                    gather(q, t, False)

        @block.scalar
        def _(act):
            for n, (_, dst, rows, cols) in enumerate(pieces):
                act.wait_ge(s_stage[n % 2], 16 * (n // 2 + 1))
                act.activation(dst[0], stage[0:rows, n % 2, 0:cols], ACT.Copy).then_inc(s_wh, 1)

            def x_hi(q):
                for t in range(QT):
                    act.wait_ge(s_t, QT * q + t + 1)
                    act.activation(xT[0][:, :, t * P:(t + 1) * P], tr[t % 2][:].rearrange("p (k s) -> p k s", k=KC),
                                   ACT.Copy).then_inc(s_th, 1)

            def hidden_hi(q, c):
                n = SCH[c][1]
                act.wait_ge(s_mul, len(SCH) * q + c + 1)
                act.activation(hid[0][0:n, c, :], h_raw[c % 2][0:n, :], ACT.Copy).then_inc(s_hh, 1)

            def turn(q, last):
                for c, (_, n) in enumerate(SCH):
                    act.wait_ge(s_gu, len(SCH) * q + c + 1)
                    act.activation(act_g[c % 2][0:n, :], gt[c % 2][0:n, :], ACT.Silu).then_inc(s_silu, 1)
                    if c:
                        hidden_hi(q, c - 1)
                hidden_hi(q, len(SCH) - 1)
                if not last:
                    x_hi(q + 1)

            x_hi(0)
            with act.Fori(0, quads - 1) as q:
                turn(q, False)
            turn(quads - 1, True)

        @block.vector
        def _(dve):
            for n, (_, dst, rows, cols) in enumerate(pieces):
                dve.wait_ge(s_wh, n + 1)
                dve.tensor_tensor(dst[1], stage[0:rows, n % 2, 0:cols], dst[0].bitcast(F32), ALU.subtract).then_inc(s_wl, 1)

            def x_lo(q):
                for t in range(QT):
                    cols = slice(t * P, (t + 1) * P)
                    dve.wait_ge(s_th, QT * q + t + 1)
                    dve.tensor_tensor(xT[1][:, :, cols], tr[t % 2][:].rearrange("p (k s) -> p k s", k=KC),
                                      xT[0][:, :, cols].bitcast(F32), ALU.subtract).then_inc(s_tl, 1)

            def routed(q, t):
                b = t % 2
                n = q * (QT // 2) + t // 2
                dve.wait_ge(s_x3[b], 16 * (n + 1))
                dve.tensor_copy(w_t[b][:], weight[:, bass.ds((q * QT + t) * TOPK, TOPK)]).then_inc(s_wt[b], 1)
                dve.wait_ge(s_wt[b], n + 1)
                for k in range(TOPK):
                    dve.wait_ge(s_yk[b][k], 16 * (n + 1))
                    dve.scalar_tensor_tensor(acc[b][:], yk[b][:, k * H:(k + 1) * H], w_t[b][:, k:k + 1], acc[b][:],
                                             ALU.mult, ALU.add).then_inc(s_acc[b], 1)
                    dve.wait_ge(s_acc[b], TOPK * n + k + 1)

            def finish(q, t, first):
                b = t % 2
                n = q * (QT // 2) + t // 2
                dve.wait_ge(s_dn, QT * q + t + 1)
                if not first:
                    dve.wait_ge(s_st[b], 16 * n)
                dve.tensor_tensor(o_sb[b][:], dn[b][:], acc[b][:], ALU.add).then_inc(s_o[b], 1)

            def turn(q, first, last):
                for c, (_, n) in enumerate(SCH):
                    dve.wait_ge(s_silu, len(SCH) * q + c + 1)
                    if not (first and c < 2):
                        dve.wait_ge(s_hl, len(SCH) * q + c - 1)
                    dve.tensor_tensor(h_raw[c % 2][0:n, :], up[c % 2][0:n, :], act_g[c % 2][0:n, :], ALU.mult).then_inc(s_mul, 1)
                    if c >= 1:
                        hidden_lo(q, c - 1, first)
                hidden_lo(q, len(SCH) - 1, first)
                if not last:
                    x_lo(q + 1)
                for t in range(QT):
                    routed(q, t)
                    finish(q, t, first and t < 2)

            def hidden_lo(q, c, first):
                n = SCH[c][1]
                dve.wait_ge(s_hh, len(SCH) * q + c + 1)
                dve.tensor_tensor(hid[1][0:n, c, :], h_raw[c % 2][0:n, :], hid[0][0:n, c, :].bitcast(F32),
                                  ALU.subtract).then_inc(s_hl, 1)

            x_lo(0)
            turn(0, True, False)
            with dve.Fori(1, quads - 1) as q:
                turn(q, False, False)
            turn(quads - 1, False, True)

        @block.tensor
        def _(pe):
            def turn_tokens(q, first):
                for t in range(QT):
                    if t == 0:
                        pe.wait_ge(s_xf, 16 * (q + 1))
                    if t >= 2:
                        pe.wait_ge(s_tl, QT * q + t - 1)
                    transpose4(pe, tr[t % 2], xf_sb[:, t, :], ident[:]).then_inc(s_t, 1)

            def hidden(q, first):
                pe.wait_ge(s_tl, QT * (q + 1))
                for c, (m, n) in enumerate(SCH):
                    if not (first and c < 2):
                        pe.wait_ge(s_mul, len(SCH) * q + c - 1)
                    for w, bank in ((sg, gt[c % 2]), (su, up[c % 2])):
                        for k in range(KC):
                            ins = matmul3(pe, bank[0:n, :], (w[0][:, k, m:m + n], w[1][:, k, m:m + n]),
                                          (xT[0][:, k, :], xT[1][:, k, :]), k == 0, k == KC - 1)
                    ins.then_inc(s_gu, 1)

            def down(q, first):
                pe.wait_ge(s_hl, len(SCH) * (q + 1))
                for t in range(QT):
                    if not (first and t < 2):
                        pe.wait_ge(s_o[t % 2], q * (QT // 2) + t // 2)
                    toks = slice(t * P, (t + 1) * P)
                    for c, (_, n) in enumerate(SCH):
                        ins = matmul3(pe, dn[t % 2][:], (hid[0][0:n, c, toks], hid[1][0:n, c, toks]),
                                      (sd[0][0:n, c, :], sd[1][0:n, c, :]), c == 0, c == len(SCH) - 1)
                    ins.then_inc(s_dn, 1)

            turn_tokens(0, True)
            pe.wait_ge(s_wl, len(pieces))

            def turn(q, first, last):
                hidden(q, first)
                if not last:
                    turn_tokens(q + 1, False)
                down(q, first)

            turn(0, True, False)
            with pe.Fori(1, quads - 1) as q:
                turn(q, False, False)
            turn(quads - 1, False, True)


_INS = ['x', 'ctx_2048', 'mask_BxS2_ik0', 'L0_attn_Wqkv', 'L0_attn_bqkv', 'L0_attn_Wo', 'L0_attn_bo', 'L0_xattn_Wq',
        'L0_xattn_bq', 'L0_xattn_Wk', 'L0_xattn_bk', 'L0_xattn_Wv', 'L0_xattn_bv', 'L0_xattn_Wo', 'L0_xattn_bo',
        'L0_xattn_ln_gamma', 'L0_xattn_ln_beta', 'L0_xattn_residual_scale', 'L0_ffn_gate_weight', 'L0_ffn_Wg',
        'L0_ffn_Wu', 'L0_ffn_Wd', 'L0_ffn_Sg', 'L0_ffn_Su', 'L0_ffn_Sd']


def _lay(name, a):
    if name == 'x':
        return a.reshape(T, H)
    if name == 'ctx_2048':
        return a.transpose(0, 2, 1).reshape(BATCH, KC, P, SEQ).transpose(0, 2, 1, 3).reshape(T, H)
    if name == 'mask_BxS2_ik0':
        return a.reshape(-1)
    if name == 'L0_xattn_residual_scale':
        return a.reshape(1)
    if name in ('L0_ffn_Wg', 'L0_ffn_Wu'):
        return a.transpose(0, 2, 1).reshape(E, KC, P, M).transpose(0, 2, 1, 3).reshape(E * P, KC * M)
    if name == 'L0_ffn_Wd':
        return a.transpose(0, 2, 1).reshape(E * M, H)
    if name.startswith('L0_xattn_W') or name.startswith('L0_ffn'):
        return a.T
    return a


def build(nc, a, out):
    with ExitStack() as ctx:
        ident = ctx.enter_context(nc.sbuf_tensor("ident", [P, P], F32))
        weight = ctx.enter_context(nc.sbuf_tensor("weight", [P, BATCH * TOPK], F32))
        slot = ctx.enter_context(nc.sbuf_tensor("slot", [P, BATCH * TOPK], U32))
        x1 = nc.dram_tensor("x1_dram", [T, H], F32, kind="Internal").ap()
        x3 = nc.dram_tensor("x3_dram", [T, H], F32, kind="Internal").ap()
        xf = nc.dram_tensor("xf_dram", [T, H], F32, kind="Internal").ap()
        table = nc.dram_tensor("table_dram", [2 * SLOTS, 1], F32, kind="Internal").ap()
        y = nc.dram_tensor("y_dram", [SLOTS, H], F32, kind="Internal").ap()
        const = dict(ident=ident)
        attention_phase(nc, False, a['x'], None, [(a['L0_attn_Wqkv'], None, 0)], a['L0_attn_Wo'],
                        [a['L0_attn_bqkv'], a['L0_attn_bo']], x1, const=const)
        n = 'L0_xattn_'
        attention_phase(nc, True, x1, a['ctx_2048'],
                        [(a[n + 'Wq'], None, 0), (a[n + 'Wk'], None, H), (a[n + 'Wv'], None, 2 * H)], a[n + 'Wo'],
                        [a[n + k] for k in ('bq', 'bk', 'bv', 'bo', 'ln_gamma', 'ln_beta', 'residual_scale')], x3,
                        route=dict(gate=a['L0_ffn_gate_weight'], mask=a['mask_BxS2_ik0'], xf=xf, table=table,
                                   weight=weight, slot=slot), const=const)
        expert_phase(nc, a['L0_ffn_Wg'], a['L0_ffn_Wu'], a['L0_ffn_Wd'], xf, table, y, ident)
        shared_phase(nc, a['L0_ffn_Sg'], a['L0_ffn_Su'], a['L0_ffn_Sd'], xf, x3, y, out, weight, slot, ident)


def kernel(**inputs):
    import numpy as _np
    import concourse.bacc as _bacc
    from concourse import mybir as _mybir
    from concourse.bass_utils import run_bass_kernel_spmd as _run

    nc = _bacc.Bacc("TRN2", target_bir_lowering=False, num_devices=1)
    arrays, args = {}, {}
    for name in _INS:
        a = _np.ascontiguousarray(_lay(name, _np.asarray(inputs[name])))
        arrays[f"in_{name}_dram"] = a
        args[name] = nc.dram_tensor(f"in_{name}_dram", a.shape, _mybir.dt.from_np(a.dtype), kind="ExternalInput").ap()
    out = nc.dram_tensor("out_0_dram", (T, H), _mybir.dt.from_np(_np.dtype('float32')), kind="ExternalOutput").ap()
    build(nc, args, out)
    r = _run(nc, [arrays], core_ids=[0])
    return r.results[0]["out_0_dram"].reshape(BATCH, SEQ, H)
```

```python
import concourse.bass as bass
from concourse import mybir
from contextlib import ExitStack

F32 = mybir.dt.float32
F32R = mybir.dt.float32r
BF16 = mybir.dt.bfloat16
I32 = mybir.dt.int32
U32 = mybir.dt.uint32
ALU = mybir.AluOpType
ACT = mybir.ActivationFunctionType
AX = mybir.AxisListType.X

P = 128
BATCH, SEQ, H = 16, 128, 512
T = BATCH * SEQ
KC = H // P
NH, HD = 16, 32
HPC = P // HD
SCALE = float(HD) ** -0.5
LN_EPS = 1e-5
LANES = 2
PAIRS = BATCH // LANES
E, TOPK, GROUPS, TOPG = 64, 6, 8, 3
GSIZE = E // GROUPS
CAP = 192
SLOTS = E * CAP
NEG = -10000.0
STAGES = 6
PEELED = 3
CLIP = 50.0
RES_MAX = 0.3


class Chain:

    def __init__(self, eng, sem):
        self.eng, self.sem, self.base, self.n, self.total = eng, sem, 0, 0, 0

    def enter(self, i, first, per):
        self.total += self.n
        self.base, self.n = i * per + (self.total - first * per), 0

    def leave(self, turns, per):
        assert self.n == per, (self.n, per)
        self.total += turns * per
        self.base, self.n = self.total, 0

    def link(self, ins):
        self.n += 1
        ins.then_inc(self.sem, 1)
        self.eng.wait_ge(self.sem, self.base + self.n)


def pipeline(eng, half, chain=None, per=0):
    half(norm=(0, 0))
    half(project=(0, 0), norm=(0, 1))

    def back(i, by, L):
        return (i - by, L) if not isinstance(i, int) or i >= by else None

    def turn(i, more=True):
        half(softmax=(i, 0), project=(i, 1), finish=back(i, 1, 1), route=back(i, 1, 0), place=back(i, 2, 1),
             norm=(i + 1, 0) if more else None)
        half(softmax=(i, 1), project=(i + 1, 0) if more else None, finish=(i, 0), route=back(i, 1, 1),
             place=back(i, 1, 0), norm=(i + 1, 1) if more else None)

    for i in range(PEELED):
        turn(i)
    with eng.Fori(PEELED, PAIRS - 1) as i:
        if chain:
            chain.enter(i, PEELED, per)
        turn(i)
    if chain:
        chain.leave(PAIRS - 1 - PEELED, per)
    turn(PAIRS - 1, False)
    half(finish=(PAIRS - 1, 1), route=(PAIRS - 1, 0), place=(PAIRS - 2, 1))
    half(place=(PAIRS - 1, 0))
    half(route=(PAIRS - 1, 1))
    half(place=(PAIRS - 1, 1))


def matmul3(pe, out, a, b, first, last):
    (ah, al), (bh, bl) = a, b
    pe.matmul(out, al, bh, start=first, stop=False)
    pe.matmul(out, ah, bl, start=False, stop=False)
    return pe.matmul(out, ah, bh, start=False, stop=last)


def transpose4(pe, bank, src, ident):
    for c in range(KC):
        ins = pe.transpose(bank[:, c * P:(c + 1) * P], src[:, c * P:(c + 1) * P], ident)
    return ins


def end_phase(nc, sems):
    nc.clear_and_free_semaphores(sems)
    nc.all_engine_barrier()


def weight_pieces(w_in, others):
    pieces = []
    for t, srcs in enumerate([w_in] + [[w] for w in others]):
        at = 0
        for src in srcs:
            for a in range(0, src.shape[1], H):
                m = min(H, src.shape[1] - a)
                pieces += [(src[k * P:(k + 1) * P, a:a + m], (t, k, at + a, m)) for k in range(KC)]
            at += src.shape[1]
    return pieces


def attention_phase(nc, cross, x_in, ctx_in, pieces, vecs, out_x, stage, loaded_before, route=None, const=None,
                    ahead=None):
    ident = const["ident"]
    with ExitStack() as ctx:
        tag = "c_" if cross else "s_"

        def sb(name, shape, dt=F32):
            return ctx.enter_context(nc.sbuf_tensor(tag + name, shape, dt))

        sems = []

        def sem(name):
            sems.append(nc.alloc_semaphore(tag + name))
            return sems[-1]

        def lanes(make, name, *a):
            return [make(f"{name}{L}", *a) for L in range(LANES)]

        ps = [ctx.enter_context(nc.psum_tensor(f"{tag}ps{L}", [P, 4, 512], F32)) for L in range(LANES)]

        wi = [sb("wi_hi", [P, KC, 3 * H], F32R), sb("wi_lo", [P, KC, 3 * H], F32R)]
        wo = [sb("wo_hi", [P, KC, H], F32R), sb("wo_lo", [P, KC, H], F32R)]
        bias_in = sb("bias_in", [P, 3 * H])
        bias_out = sb("bias_out", [P, H])
        minus_half = sb("minus_half", [P, 1])
        ready_mark = sb("ready_mark", [P, 1])
        scratch = sb("scratch", [P, 1])
        scratch_p = sb("scratch_p", [P, LANES])
        eps = sb("eps", [P, 1])
        if cross:
            gate = [sb("gate_hi", [P, KC, E], F32R), sb("gate_lo", [P, KC, E], F32R)]
            gamma = sb("gamma", [P, H])
            beta = sb("beta", [P, H])
            rs = sb("rs", [P, 1])
            rs2 = sb("rs2", [P, 1])
            imask = sb("imask", [P, BATCH], I32)
            attend = sb("attend", [P, BATCH])
            not_bias = sb("not_bias", [P, BATCH])
            exp_scale = lanes(sb, "exp_scale", [P, 1])
            exp_bias = lanes(sb, "exp_bias", [P, 1])
            iota8 = sb("iota8", [P, GROUPS])
            iota64 = sb("iota64", [P, E])
            before_me = sb("before_me", [P, P], BF16)
            all_ones = sb("all_ones", [P, P], BF16)
            diag_pos = sb("diag_pos", [P, P], BF16)
            rowid = sb("rowid", [P, 1])
            token = lanes(sb, "token", [P, 1])
            dump = lanes(sb, "dump", [P, TOPK])
            tbase = lanes(sb, "tbase", [E, 1])
            count = sb("count", [P, E])
            last_tok = sb("last_tok", [E, 1])
            zero_row = sb("zero_row", [E, CAP])
            gmax = lanes(sb, "gmax", [P, GROUPS])
            gtop = lanes(sb, "gtop", [P, 8])
            gidx = lanes(sb, "gidx", [P, 8], U32)
            gidf = lanes(sb, "gidf", [P, 8])
            gone = lanes(sb, "gone", [P, TOPG, GROUPS])
            gmask = lanes(sb, "gmask", [P, GROUPS])
            lneg = lanes(sb, "lneg", [P, 1])
            lsum = lanes(sb, "lsum", [P, 1])
            prob = lanes(sb, "prob", [P, E])
            top = lanes(sb, "top", [P, 8])
            tidx = lanes(sb, "tidx", [P, 8], U32)
            tidf = lanes(sb, "tidf", [P, 8])
            onehot = lanes(sb, "onehot", [P, TOPK, E])
            chosen = lanes(sb, "chosen", [P, E], BF16)
            posn = lanes(sb, "posn", [P, E])
            posk = lanes(sb, "posk", [P, TOPK])
            over = lanes(sb, "over", [P, TOPK])
            slot = lanes(sb, "slot", [P, TOPK])
            wslot = lanes(sb, "wslot", [P, TOPK], U32)
            lmax = lanes(sb, "lmax", [E, 1])
            lpos = lanes(sb, "lpos", [E, 1])
        else:
            tri_scale = sb("tri_scale", [P, P])
            tri_neg = sb("tri_neg", [P, P])

        x_sb = lanes(sb, "x", [P, H])
        xn = lanes(sb, "xn", [P, H])
        stats = lanes(sb, "stats", [P, 6])
        mv = lanes(sb, "mv", [P, 2])
        rstd = lanes(sb, "rstd", [P, 1])
        xnT = [[sb(f"xnT_hi{L}", [P, H], F32R), sb(f"xnT_lo{L}", [P, H], F32R)] for L in range(LANES)]
        q_sb = lanes(sb, "q", [P, H])
        k_sb = lanes(sb, "k", [P, H])
        v_sb = lanes(sb, "v", [P, NH, HD + 1])
        plain = lanes(sb, "plain", [P, H])
        blocks = lanes(sb, "blocks", [P, KC, HPC, SEQ])
        prb = lanes(sb, "prb", [P, NH, SEQ])
        nmax = lanes(sb, "nmax", [P, NH])
        rsum = lanes(sb, "rsum", [P, NH])
        rsum2 = lanes(sb, "rsum2", [P, NH])
        attn = lanes(sb, "attn", [P, H])
        aT = [[sb(f"aT_hi{L}", [P, H], F32R), sb(f"aT_lo{L}", [P, H], F32R)] for L in range(LANES)]
        xb = lanes(sb, "xb", [P, H])
        x1 = lanes(sb, "x1", [P, H])
        if cross:
            ctx_sb = lanes(sb, "ctx", [P, H])
            cT = [[sb(f"cT_hi{L}", [P, H], F32R), sb(f"cT_lo{L}", [P, H], F32R)] for L in range(LANES)]
            dlt = lanes(sb, "dlt", [P, H])
            fac = lanes(sb, "fac", [P, 1])
            xf = lanes(sb, "xf", [P, H])
            xfT = xnT

        s_vec = sem("vec_loaded")
        s_stage = [sem(f"stage_loaded{n}") for n in range(STAGES)]
        s_hi = sem("weight_hi")
        s_lo = sem("weight_lo")
        s_const = sem("const_ready")
        s_ident = sem("ident_ready")
        s_x = lanes(sem, "x_loaded")
        s_var = lanes(sem, "var_ready")
        s_rstd = lanes(sem, "rstd_ready")
        s_xn = lanes(sem, "xn_ready")
        s_xb = lanes(sem, "xb_ready")
        s_t1 = lanes(sem, "xnT_in_psum")
        s_t1h = lanes(sem, "xnT_hi_ready")
        s_t1l = lanes(sem, "xnT_lo_ready")
        s_m1 = lanes(sem, "qkv_in_psum")
        s_qk = lanes(sem, "qk_ready")
        s_v = lanes(sem, "v_ready")
        s_t2 = lanes(sem, "qkT_in_psum")
        s_plain = lanes(sem, "plain_ready")
        s_blocks = lanes(sem, "blocks_ready")
        s_sc = lanes(sem, "scores_in_psum")
        s_max = lanes(sem, "masked_ready")
        s_exp = lanes(sem, "exp_ready")
        s_pT = lanes(sem, "probsT_in_psum")
        s_pTs = lanes(sem, "probsT_ready")
        s_pv = lanes(sem, "pv_in_psum")
        s_at = lanes(sem, "attn_ready")
        s_t4 = lanes(sem, "attnT_in_psum")
        s_t4h = lanes(sem, "attnT_hi_ready")
        s_t4l = lanes(sem, "attnT_lo_ready")
        s_o = lanes(sem, "o_in_psum")
        s_of = lanes(sem, "o_bank_free")
        s_x1 = lanes(sem, "x1_ready")
        s_st = lanes(sem, "x1_stored")
        s_dve = sem("dve_step")
        s_pool = sem("pool_step")
        if cross:
            s_c = lanes(sem, "ctx_loaded")
            s_ch = lanes(sem, "ctx_hi_ready")
            s_cl = lanes(sem, "ctx_lo_ready")
            s_var2 = lanes(sem, "delta_var_ready")
            s_fac = lanes(sem, "delta_factor_ready")
            s_dn = lanes(sem, "delta_normed")
            s_var3 = lanes(sem, "x3_var_ready")
            s_rstd3 = lanes(sem, "x3_rstd_ready")
            s_xf = lanes(sem, "xf_ready")
            s_stf = lanes(sem, "xf_stored")
            s_t5 = lanes(sem, "xfT_in_psum")
            s_t5h = lanes(sem, "xfT_hi_ready")
            s_t5l = lanes(sem, "xfT_lo_ready")
            s_lg = lanes(sem, "logits_in_psum")
            s_lm = lanes(sem, "logit_max_ready")
            s_le = lanes(sem, "logit_exp_ready")
            s_choice = lanes(sem, "choice_ready")
            s_pos = lanes(sem, "positions_in_psum")
            s_posd = lanes(sem, "positions_read")
            s_posk = lanes(sem, "positions_ready")
            s_ws = lanes(sem, "write_slots_ready")
            s_sct = lanes(sem, "tokens_scattered")
            s_mask = sem("mask_loaded")
            s_last = sem("last_tokens_ready")
            s_lst = sem("last_tokens_stored")

        def split_piece(n):
            t, k, a, m = pieces[n][1]
            hi, lo = (wi, wo, gate)[t] if cross else (wi, wo)[t]
            return (hi[:, k, a:a + m], lo[:, k, a:a + m]), m

        before = STAGES if loaded_before else 0

        FIRST_PIECES = KC

        ctx.callback(end_phase, nc, sems)
        block = ctx.enter_context(nc.Block())

        @block.sync
        def _(sp):
            def half(softmax=None, project=None, finish=None, route=None, place=None, norm=None):
                if norm:
                    i, L = norm
                    b = i * LANES + L
                    if not isinstance(i, int) or i:
                        sp.wait_ge(s_xn[L], i)
                        sp.wait_ge(s_xb[L], i)
                        if cross:
                            sp.wait_ge(s_cl[L], i)
                    sp.dma_start(x_sb[L][:], x_in[bass.ds(b * P, P), :]).then_inc(s_x[L], 16)
                    if cross:
                        sp.dma_start(ctx_sb[L][:], ctx_in[bass.ds(b * P, P), :]).then_inc(s_c[L], 16)
                if project and not softmax:
                    for n in range(before, len(pieces)):
                        if n >= STAGES:
                            sp.wait_ge(s_lo, n - STAGES + 1)
                        src, (_, _, _, m) = pieces[n]
                        sp.dma_start(stage[:, n % STAGES, 0:m], src).then_inc(s_stage[n % STAGES], 16)
                if finish:
                    i, L = finish
                    b = i * LANES + L
                    sp.wait_ge(s_x1[L], i + 1)
                    sp.dma_start(out_x[bass.ds(b * P, P), :], x1[L][:]).then_inc(s_st[L], 16)
                    if cross:
                        sp.wait_ge(s_xf[L], i + 1)
                        sp.dma_start(xf_out[bass.ds(b * P, P), :], xf[L][:]).then_inc(s_stf[L], 16)

            if cross:
                sp.dma_start(imask[:], route["mask"]).then_inc(s_mask, 16)
                xf_out = route["xf"]
            pipeline(sp, half)
            if ahead:
                for n in range(STAGES):
                    sp.dma_start(stage[:, n, :], ahead[0][n][0]).then_inc(ahead[1], 16)
            if cross:
                sp.wait_ge(s_last, 1)
                for L in range(LANES):
                    sp.wait_ge(s_sct[L], 16 + 16 * TOPK * PAIRS)
                table = route["table"][0:SLOTS, :].rearrange("(e c) o -> e (c o)", c=CAP)
                sp.dma_start(table[:, CAP - 1:CAP], last_tok[:], allow_slow_non_contiguous=True).then_inc(s_lst, 16)
                sp.wait_ge(s_lst, 16)
            for L in range(LANES):
                sp.wait_ge(s_st[L], 16 * PAIRS)
                if cross:
                    sp.wait_ge(s_stf[L], 16 * PAIRS)

        @block.gpsimd
        def _(pool):
            chain = Chain(pool, s_pool)
            chain.link(pool.memset(minus_half[:], -0.5))
            chain.link(pool.memset(eps[:], LN_EPS))
            if not cross:
                chain.link(pool.memset(ident[:], 0.0))
                chain.link(pool.affine_select(out=ident[:], in_=ident[:], pattern=[[-1, P]], compare_op=ALU.not_equal,
                                              fill=1.0, base=0, channel_multiplier=1))
                pool.memset(scratch_p[:], 0.0).then_inc(s_ident, 1)

            def constants():
                for L in range(LANES):
                    chain.link(pool.memset(blocks[L][:], 0.0))
                    chain.link(pool.memset(v_sb[L][:, :, HD:HD + 1], 1.0))
                if not cross:
                    chain.link(pool.memset(tri_scale[:], SCALE))
                    chain.link(pool.affine_select(out=tri_scale[:], in_=tri_scale[:], pattern=[[-1, P]],
                                                  compare_op=ALU.is_ge, fill=0.0, base=0, channel_multiplier=1))
                    chain.link(pool.memset(tri_neg[:], 0.0))
                    chain.link(pool.affine_select(out=tri_neg[:], in_=tri_neg[:], pattern=[[-1, P]],
                                                  compare_op=ALU.is_ge, fill=NEG, base=0, channel_multiplier=1))
                else:
                    lk = chain.link
                    lk(pool.iota(iota8[:], pattern=[[1, GROUPS]], base=0, channel_multiplier=0,
                                 allow_small_or_imprecise_dtypes=True))
                    lk(pool.iota(iota64[:], pattern=[[1, E]], base=0, channel_multiplier=0,
                                 allow_small_or_imprecise_dtypes=True))
                    lk(pool.memset(all_ones[:], 1.0))
                    lk(pool.affine_select(out=before_me[:], in_=all_ones[:], pattern=[[1, P]],
                                          compare_op=ALU.is_gt, fill=0.0, base=0, channel_multiplier=-1))
                    lk(pool.iota(diag_pos[:], pattern=[[1, P]], base=1, channel_multiplier=0,
                                 allow_small_or_imprecise_dtypes=True))
                    lk(pool.affine_select(out=diag_pos[:], in_=diag_pos[:], pattern=[[1, P]],
                                          compare_op=ALU.is_equal, fill=0.0, base=0, channel_multiplier=-1))
                    lk(pool.memset(count[:], 0.0))
                    lk(pool.memset(last_tok[:], 0.0))
                    lk(pool.memset(zero_row[:], 0.0))
                    for L in range(LANES):
                        lk(pool.iota(token[L][:], pattern=[[0, 1]], base=(L - LANES) * P, channel_multiplier=1,
                                     allow_small_or_imprecise_dtypes=True))
                        lk(pool.iota(dump[L][:], pattern=[[1, TOPK]], base=SLOTS + (L - LANES) * P * TOPK,
                                     channel_multiplier=TOPK, allow_small_or_imprecise_dtypes=True))
                        lk(pool.memset(tbase[L][:], float((L - LANES) * P - 1)))
                    table = route["table"][0:SLOTS, :].rearrange("(e c) o -> e (c o)", c=CAP)
                    half = E // LANES
                    for L in range(LANES):
                        rows = slice(L * half, (L + 1) * half)
                        pool.dma_start(table[rows, :], zero_row[rows, :]).then_inc(s_sct[L], 16)
                    for L in range(LANES):
                        pool.wait_ge(s_sct[L], 16)
                pool.wait_ge(s_vec, 16 * len(vecs))
                if cross:
                    chain.link(pool.tensor_scalar(rs[:], rs[:], 0.0, RES_MAX, ALU.max, ALU.min))
                    chain.link(pool.tensor_tensor(rs2[:], rs[:], rs[:], ALU.mult))
                pool.memset(ready_mark[:], 0.0).then_inc(s_const, 1)

            def inv_std(L, s_ready, i, s_done, scaled=False):
                pool.wait_ge(s_ready[L], i + 1)
                dst = fac[L] if scaled else rstd[L]
                if scaled:
                    chain.link(pool.tensor_tensor(dst[:], mv[L][:, 1:2], rs2[:], ALU.mult))
                    chain.link(pool.tensor_tensor(dst[:], dst[:], eps[:], ALU.add))
                    chain.link(pool.tensor_tensor(dst[:], dst[:], minus_half[:], ALU.pow))
                    pool.tensor_tensor(dst[:], dst[:], rs[:], ALU.mult).then_inc(s_done[L], 1)
                else:
                    chain.link(pool.tensor_tensor(dst[:], mv[L][:, 1:2], eps[:], ALU.add))
                    pool.tensor_tensor(dst[:], dst[:], minus_half[:], ALU.pow).then_inc(s_done[L], 1)

            def residual(i, L):
                pool.wait_ge(s_x[L], 16 * (i + 1))
                pool.wait_ge(s_x1[L], i)
                pool.tensor_tensor(xb[L][:], x_sb[L][:], (beta if cross else bias_out)[:], ALU.add).then_inc(s_xb[L], 1)

            def split_ctx(i, L):
                pool.wait_ge(s_ch[L], i + 1)
                pool.wait_ge(s_m1[L], 3 * i)
                pool.tensor_tensor(cT[L][1][:], ctx_sb[L][:], cT[L][0][:].bitcast(F32), ALU.subtract).then_inc(s_cl[L], 1)

            def scatter(i, L):
                pool.wait_ge(s_ws[L], i + 1)
                if not isinstance(i, int):
                    pool.tensor_tensor(scratch_p[:, L:L + 1], eps[:], eps[:], ALU.mult)
                for k in range(TOPK):
                    pool.indirect_dma_start(out=route["table"], in_=token[L][:], in_offset=None,
                                            out_offset=bass.IndirectOffsetOnAxis(ap=wslot[L][:, k:k + 1], axis=0)
                                            ).then_inc(s_sct[L], 16)

            def half(softmax=None, project=None, finish=None, route=None, place=None, norm=None):
                if cross and project:
                    split_ctx(*project)
                if project and not softmax:
                    constants()
                if cross and finish:
                    i, L = finish
                    inv_std(L, s_var2, i, s_fac, scaled=True)
                    inv_std(L, s_var3, i, s_rstd3)
                if norm:
                    i, L = norm
                    inv_std(L, s_var, i, s_rstd)
                if project:
                    residual(*project)
                if cross and place:
                    scatter(*place)

            pipeline(pool, half, chain, LANES * (1 + 3 + 1 if cross else 1))
        @block.scalar
        def _(act):
            def load_vectors(eng):
                dsts = (bias_in[:, 0:H], bias_in[:, H:2 * H], bias_in[:, 2 * H:3 * H], bias_out[:], gamma[:], beta[:],
                        rs[:]) if cross else (bias_in[:], bias_out[:])
                for src, dst in zip(vecs, dsts):
                    eng.dma_start(dst, src.partition_broadcast(P)).then_inc(s_vec, 16)

            load_vectors(act)

            def split_weights(a, b):
                for n in range(a, b):
                    (hi, _), m = split_piece(n)
                    if n < before:
                        act.wait_ge(loaded_before, 16 * before)
                    else:
                        act.wait_ge(s_stage[n % STAGES], 16 * (n // STAGES + (0 if before else 1)))
                    act.activation(hi, stage[:, n % STAGES, 0:m], ACT.Copy).then_inc(s_hi, 1)

            def split_hi(bank, dst, s_in, i, s_done, L):
                act.wait_ge(s_in[L], i + 1)
                act.activation(dst[L][0][:], ps[L][:, bank, :], ACT.Copy).then_inc(s_done[L], 1)

            def exps(i, c, L):
                act.wait_ge(s_max[L], KC * i + c + 1)
                heads = slice(c * HPC, (c + 1) * HPC)
                if cross:
                    ins = act.activation(prb[L][:, heads, :], prb[L][:, heads, :], ACT.Exp, scale=exp_scale[L][:],
                                         bias=exp_bias[L][:])
                else:
                    for h in range(c * HPC, (c + 1) * HPC):
                        ins = act.activation(prb[L][:, h, :], prb[L][:, h, :], ACT.Exp, bias=nmax[L][:, h:h + 1])
                ins.then_inc(s_exp[L], 1)

            def copy_probsT(i, c, L):
                act.wait_ge(s_pT[L], KC * i + c + 1)
                act.activation(prb[L][:, c * HPC:(c + 1) * HPC, :],
                               ps[L][:, c, :].rearrange("p (h s) -> p h s", h=HPC), ACT.Copy).then_inc(s_pTs[L], 1)

            def scores_operands(i, L):
                act.wait_ge(s_t2[L], 2 * i + 2)
                for j in range(HPC if cross else 2):
                    r = slice(j * HD, (j + 1) * HD)
                    ins = act.activation(blocks[L][r, :, j, :], ps[L][r, 0, :].rearrange("p (c s) -> p c s", c=KC), ACT.Copy)
                ins.then_inc(s_blocks[L], 1)
                act.activation(plain[L][:], ps[L][:, 3, :], ACT.Copy).then_inc(s_plain[L], 1)

            def half(softmax=None, project=None, finish=None, route=None, place=None, norm=None):
                starting = project and not softmax
                if cross and route:
                    route_exp(*route)
                if finish:
                    i, L = finish
                    split_hi(2, aT, s_t4, i, s_t4h, L)
                if starting:
                    split_weights(0, FIRST_PIECES)
                if project:
                    i, L = project
                    if cross:
                        act.wait_ge(s_c[L], 16 * (i + 1))
                        act.wait_ge(s_m1[L], 3 * i)
                        act.activation(cT[L][0][:], ctx_sb[L][:], ACT.Copy).then_inc(s_ch[L], 1)
                    split_hi(1, xnT, s_t1, i, s_t1h, L)
                if starting:
                    split_weights(FIRST_PIECES, len(pieces))
                if softmax:
                    i, L = softmax
                    if cross:
                        for c in range(KC):
                            exps(i, c, L)
                    else:
                        for c in range(3):
                            exps(i, c, L)
                        for c in range(2):
                            copy_probsT(i, c, L)
                        exps(i, 3, L)
                        for c in range(2, KC):
                            copy_probsT(i, c, L)
                if project:
                    scores_operands(*project)
                if cross and finish:
                    route_hi(*finish)

            def route_hi(i, L):
                split_hi(2, xfT, s_t5, i, s_t5h, L)

            def route_exp(i, L):
                act.wait_ge(s_lm[L], i + 1)
                act.activation(prob[L][:], ps[L][:, 1, 0:E], ACT.Exp, bias=lneg[L][:], accum_out=lsum[L][:]).then_inc(s_le[L], 1)

            pipeline(act, half)

        @block.vector
        def _(dve):
            chain = Chain(dve, s_dve)
            link = chain.link

            def split_weights(a, b):
                for n in range(a, b):
                    (hi, lo), m = split_piece(n)
                    dve.wait_ge(s_hi, n + 1)
                    dve.tensor_tensor(lo, stage[:, n % STAGES, 0:m], hi.bitcast(F32), ALU.subtract).then_inc(s_lo, 1)

            if cross:
                dve.wait_ge(s_mask, 16)
                link(dve.tensor_scalar(attend[:], imask[:], 0.5, None, ALU.is_gt))
                link(dve.tensor_scalar(not_bias[:], attend[:], 1.0, CLIP, ALU.subtract, ALU.mult))
                link(dve.tensor_scalar(attend[:], attend[:], SCALE, None, ALU.mult))

            def step_aside():
                dve.memset(scratch[:], 0.0)

            def norm_stats(src, L, s_done):
                link(dve.bn_stats(stats[L][:], src))
                step_aside()
                dve.bn_aggr(mv[L][:], stats[L][:]).then_inc(s_done[L], 1)

            def layernorm(i, L):
                dve.wait_ge(s_x[L], 16 * (i + 1))
                norm_stats(x_sb[L][:], L, s_var)

            def normed(i, L):
                dve.wait_ge(s_rstd[L], i + 1)
                dve.tensor_scalar(xn[L][:], x_sb[L][:], mv[L][:, 0:1], rstd[L][:, 0:1], ALU.subtract,
                                  ALU.mult).then_inc(s_xn[L], 1)

            def split_lo(bank, dst, s_hi_ready, i, s_done, L):
                dve.wait_ge(s_hi_ready[L], i + 1)
                dve.tensor_tensor(dst[L][1][:], ps[L][:, bank, :], dst[L][0][:].bitcast(F32), ALU.subtract).then_inc(s_done[L], 1)

            def qkv(i, L, n):
                dst = (q_sb[L][:], k_sb[L][:], v_sb[L][:, :, 0:HD])[n]
                dve.wait_ge(s_m1[L], 3 * i + n + 1)
                src, b = ps[L][:, n, :], bias_in[:, n * H:(n + 1) * H]
                if n == 2:
                    src, b = src.rearrange("p (h d) -> p h d", d=HD), b.rearrange("p (h d) -> p h d", d=HD)
                dve.tensor_tensor(dst, src, b, ALU.add).then_inc((s_qk if n < 2 else s_v)[L], 1)

            def scores_operands(i, L):
                dve.wait_ge(s_t2[L], 2 * i + 2)
                for j in range(2, HPC):
                    r = slice(j * HD, (j + 1) * HD)
                    ins = dve.tensor_copy(blocks[L][r, :, j, :], ps[L][r, 0, :].rearrange("p (c s) -> p c s", c=KC))
                ins.then_inc(s_blocks[L], 1)

            def mask(i, c, L):
                dve.wait_ge(s_sc[L], KC * i + c + 1)
                heads = slice(c * HPC, (c + 1) * HPC)
                out = prb[L][:, heads, :]
                src = ps[L][:, c, :].rearrange("p (h s) -> p h s", h=HPC)
                if cross:
                    if c == 0:
                        b = i * LANES + L
                        dve.tensor_copy(exp_scale[L][:], attend[:, bass.ds(b, 1)])
                        dve.tensor_copy(exp_bias[L][:], not_bias[:, bass.ds(b, 1)])
                    dve.tensor_scalar(out, src, -CLIP / SCALE, CLIP / SCALE, ALU.max, ALU.min).then_inc(s_max[L], 1)
                else:
                    link(dve.tensor_tensor(out, src, tri_scale[:].unsqueeze(1).broadcast_to([P, HPC, SEQ]), ALU.mult))
                    link(dve.tensor_tensor(out, out, tri_neg[:].unsqueeze(1).broadcast_to([P, HPC, SEQ]), ALU.add))
                    dve.tensor_reduce(nmax[L][:, heads], out, AX, ALU.max, negate=True).then_inc(s_max[L], 1)

            def attention_out(i, L):
                dve.wait_ge(s_pv[L], i + 1)
                both = ps[L][:, 0:2, 0:NH // 2 * (HD + 1)].rearrange("p b (h d) -> p b h d", d=HD + 1)
                total = both[:, :, :, HD]
                r = rsum[L][:].rearrange("p (b h) -> p b h", b=2)
                if cross:
                    r2 = rsum2[L][:].rearrange("p (b h) -> p b h", b=2)
                    link(dve.tensor_scalar(r2, total, 1e-8, None, ALU.mult))
                    link(dve.tensor_tensor(r2, r2, total, ALU.add))
                    total = r2
                link(dve.reciprocal(r, total))
                dve.tensor_tensor(attn[L][:].rearrange("p (b h d) -> p b h d", b=2, d=HD), both[:, :, :, 0:HD],
                                  r.unsqueeze(3).broadcast_to([P, 2, NH // 2, HD]), ALU.mult).then_inc(s_at[L], 1)

            def output(i, L):
                dve.wait_ge(s_o[L], i + 1)
                dve.wait_ge(s_xb[L], i + 1)
                dve.wait_ge(s_st[L], 16 * i)
                if not cross:
                    dve.tensor_tensor(x1[L][:], ps[L][:, 3, :], xb[L][:], ALU.add).then_inc(s_x1[L], 1)
                else:
                    dve.tensor_tensor(dlt[L][:], ps[L][:, 3, :], bias_out[:], ALU.add).then_inc(s_of[L], 1)
                    dve.wait_ge(s_of[L], i + 1)
                    norm_stats(dlt[L][:], L, s_var2)

            def delta(i, L):
                dve.wait_ge(s_fac[L], i + 1)
                link(dve.scalar_tensor_tensor(dlt[L][:], dlt[L][:], mv[L][:, 0:1], gamma[:], ALU.subtract, ALU.mult))
                dve.scalar_tensor_tensor(x1[L][:], dlt[L][:], fac[L][:, 0:1], xb[L][:], ALU.mult,
                                         ALU.add).then_inc(s_x1[L], 1)
                dve.wait_ge(s_x1[L], i + 1)
                norm_stats(x1[L][:], L, s_var3)

            def final_norm(i, L):
                dve.wait_ge(s_rstd3[L], i + 1)
                dve.wait_ge(s_stf[L], 16 * i)
                dve.wait_ge(s_t5[L], i)
                dve.tensor_scalar(xf[L][:], x1[L][:], mv[L][:, 0:1], rstd[L][:, 0:1], ALU.subtract,
                                  ALU.mult).then_inc(s_xf[L], 1)

            def route_max(i, L):
                dve.wait_ge(s_lg[L], i + 1)
                dve.tensor_reduce(lneg[L][:], ps[L][:, 1, 0:E], AX, ALU.max, negate=True).then_inc(s_lm[L], 1)

            def choose_groups(i, L):
                dve.wait_ge(s_le[L], i + 1)
                link(dve.reciprocal(lsum[L][:], lsum[L][:]))
                link(dve.tensor_scalar(prob[L][:], prob[L][:], lsum[L][:, 0:1], None, ALU.mult))
                grouped = prob[L][:].rearrange("p (g n) -> p g n", g=GROUPS)
                link(dve.tensor_reduce(gmax[L][:], grouped, AX, ALU.max))
                step_aside()
                link(dve.max(gtop[L][:], gmax[L][:]))
                step_aside()
                link(dve.max_index(gidx[L][:], gtop[L][:], gmax[L][:]))
                link(dve.tensor_copy(gidf[L][:], gidx[L][:]))
                link(dve.tensor_tensor(gone[L][:], iota8[:].unsqueeze(1).broadcast_to([P, TOPG, GROUPS]),
                                       gidf[L][:, 0:TOPG].unsqueeze(2).broadcast_to([P, TOPG, GROUPS]), ALU.is_equal))
                link(dve.tensor_reduce(gmask[L][:], gone[L][:].rearrange("p k g -> p g k"), AX, ALU.add))
                link(dve.tensor_tensor(grouped, grouped, gmask[L][:].unsqueeze(2).broadcast_to([P, GROUPS, GSIZE]), ALU.mult))

            def choose_experts(i, L):
                b = i * LANES + L
                step_aside()
                link(dve.max(top[L][:], prob[L][:]))
                step_aside()
                link(dve.max_index(tidx[L][:], top[L][:], prob[L][:]))
                link(dve.tensor_copy(tidf[L][:], tidx[L][:]))
                dve.tensor_copy(route["weight"][:, bass.ds(b * TOPK, TOPK)], top[L][:, 0:TOPK])
                link(dve.tensor_tensor(onehot[L][:], iota64[:].unsqueeze(1).broadcast_to([P, TOPK, E]),
                                       tidf[L][:, 0:TOPK].unsqueeze(2).broadcast_to([P, TOPK, E]), ALU.is_equal))
                with nc.allow_low_precision(reason="zeros and a single one are summed"):
                    dve.tensor_reduce(chosen[L][:], onehot[L][:].rearrange("p k e -> p e k"), AX, ALU.add).then_inc(s_choice[L], 1)

            def route_positions(i, L):
                dve.wait_ge(s_pos[L], i + 1)
                link(dve.tensor_tensor(posn[L][:], ps[L][:, 3, 0:E], count[:], ALU.add))
                link(dve.tensor_tensor(count[:], count[:], ps[L][:, 3, E:2 * E], ALU.add))
                dve.tensor_reduce(lmax[L][:], ps[L][0:E, 3, P:2 * P], AX, ALU.max).then_inc(s_posd[L], 1)
                link(dve.tensor_tensor(onehot[L][:], onehot[L][:], posn[L][:].unsqueeze(1).broadcast_to([P, TOPK, E]), ALU.mult))
                dve.tensor_reduce(posk[L][:], onehot[L][:], AX, ALU.add).then_inc(s_posk[L], 1)

            def place_tokens(i, L):
                b = i * LANES + L
                dve.wait_ge(s_posk[L], i + 1)
                dve.wait_ge(s_sct[L], 16 * TOPK * i + 16)
                dve.tensor_scalar(token[L][:], token[L][:], float(LANES * P), None, ALU.add)
                dve.tensor_scalar(dump[L][:], dump[L][:], float(LANES * P * TOPK), None, ALU.add)
                dve.tensor_scalar(tbase[L][:], tbase[L][:], float(LANES * P), None, ALU.add)
                dve.tensor_scalar(over[L][:], posk[L][:], float(CAP - 1), None, ALU.is_ge)
                link(dve.tensor_scalar(posk[L][:], posk[L][:], float(CAP - 1), None, ALU.min))
                dve.tensor_tensor(lpos[L][:], lmax[L][:], tbase[L][:], ALU.add)
                link(dve.scalar_tensor_tensor(slot[L][:], tidf[L][:, 0:TOPK], float(CAP), posk[L][:], ALU.mult, ALU.add))
                dve.scalar_tensor_tensor(lmax[L][:], lmax[L][:], 0.0, lpos[L][:], ALU.is_gt, ALU.mult)
                dve.tensor_copy(route["slot"][:, bass.ds(b * TOPK, TOPK)], slot[L][:])
                link(dve.tensor_tensor(posk[L][:], dump[L][:], slot[L][:], ALU.subtract))
                dve.tensor_tensor(last_tok[:], last_tok[:], lmax[L][:], ALU.max)
                link(dve.tensor_tensor(posk[L][:], posk[L][:], over[L][:], ALU.mult))
                dve.tensor_tensor(wslot[L][:], slot[L][:], posk[L][:], ALU.add).then_inc(s_ws[L], 1)

            def half(softmax=None, project=None, finish=None, route=None, place=None, norm=None):
                starting = project and not softmax
                if cross and route:
                    route_max(*route)
                if finish:
                    i, L = finish
                    split_lo(2, aT, s_t4h, i, s_t4l, L)
                if softmax:
                    i, L = softmax
                    mask(i, 0, L)
                if starting:
                    split_weights(0, FIRST_PIECES)
                if project:
                    i, L = project
                    split_lo(1, xnT, s_t1h, i, s_t1l, L)
                if starting:
                    split_weights(FIRST_PIECES, len(pieces))
                    dve.wait_ge(s_const, 1)
                if softmax:
                    i, L = softmax
                    mask(i, 1, L)
                if cross and route:
                    choose_groups(*route)
                if finish:
                    output(*finish)
                if softmax:
                    i, L = softmax
                    mask(i, 2, L)
                    mask(i, 3, L)
                if cross and place:
                    place_tokens(*place)
                if project:
                    i, L = project
                    qkv(i, L, 0)
                if cross and finish:
                    delta(*finish)
                if project:
                    qkv(i, L, 1)
                if norm:
                    layernorm(*norm)
                if cross and finish:
                    final_norm(*finish)
                if project:
                    i, L = project
                    qkv(i, L, 2)
                if norm:
                    normed(*norm)
                if cross and route:
                    choose_experts(*route)
                if project and not cross:
                    scores_operands(*project)
                if cross and finish:
                    i, L = finish
                    split_lo(2, xfT, s_t5h, i, s_t5l, L)
                if softmax:
                    attention_out(*softmax)
                if cross and route:
                    route_positions(*route)

            pipeline(dve, half, chain, LANES * (3 + 1 + 1 + 2 + 12 + 8 if cross else 2 * KC + 1 + 1))
            if cross:
                dve.tensor_copy(last_tok[:], last_tok[:]).then_inc(s_last, 1)

        @block.tensor
        def _(pe):
            def accumulate(bank, i, L, x, w, cols):
                for k in range(KC):
                    ks = slice(k * P, (k + 1) * P)
                    ins = matmul3(pe, ps[L][:, bank, 0:cols.stop - cols.start], (x[0][:, ks], x[1][:, ks]),
                                  (w[0][:, k, cols], w[1][:, k, cols]), k == 0, k == KC - 1)
                return ins

            def route_turn(i, L):
                pe.wait_ge(s_xf[L], i + 1)
                transpose4(pe, ps[L][:, 2, :], xf[L][:], ident[:]).then_inc(s_t5[L], 1)

            def route_logits(i, L):
                pe.wait_ge(s_t5l[L], i + 1)
                accumulate(1, i, L, xfT[L], gate, slice(0, E)).then_inc(s_lg[L], 1)

            def route_count(i, L):
                pe.wait_ge(s_choice[L], i + 1)
                pe.matmul(ps[L][:, 3, 0:E], before_me[:], chosen[L][:], start=True, stop=True)
                pe.matmul(ps[L][:, 3, E:2 * E], all_ones[:], chosen[L][:], start=True, stop=True)
                pe.matmul(ps[L][0:E, 3, P:2 * P], chosen[L][:], diag_pos[:], start=True, stop=True).then_inc(s_pos[L], 1)

            def scores(i, c, L):
                if c == 0:
                    pe.wait_ge(s_blocks[L], i + 1 if cross else 2 * i + 2)
                    pe.wait_ge(s_plain[L], i + 1)
                if c == 1 and cross:
                    pe.wait_ge(s_le[L], i)
                if c == 2:
                    pe.wait_ge(s_v[L], i + 1)
                pe.matmul(ps[L][:, c, :], plain[L][:, c * P:(c + 1) * P], blocks[L][:, c, :, :], start=True,
                          stop=True).then_inc(s_sc[L], 1)

            def project_in(i, L, n):
                pe.wait_ge(s_t1l[L], i + 1)
                if cross:
                    pe.wait_ge(s_cl[L], i + 1)
                accumulate(n, i, L, cT[L] if cross and n else xnT[L], wi, slice(n * H, (n + 1) * H)).then_inc(s_m1[L], 1)

            def probsT(i, c, L):
                pe.wait_ge(s_exp[L], KC * i + c + 1)
                for j in range(HPC):
                    ins = pe.transpose(ps[L][:, c, j * P:(j + 1) * P], prb[L][:, c * HPC + j, :], ident[:])
                ins.then_inc(s_pT[L], 1)

            def attend_v(i, L):
                for c in range(KC):
                    pe.wait_ge((s_exp if cross else s_pTs)[L], KC * i + max(c + 1, 2))
                    for h in range(c * HPC, (c + 1) * HPC):
                        at = h % (NH // 2) * (HD + 1)
                        ins = pe.matmul(ps[L][:, h // (NH // 2), at:at + HD + 1], prb[L][:, h, :], v_sb[L][:, h, :],
                                        start=True, stop=True)
                ins.then_inc(s_pv[L], 1)

            def half(softmax=None, project=None, finish=None, route=None, place=None, norm=None):
                starting = project and not softmax
                if softmax:
                    i, L = softmax
                    scores(i, 0, L)
                if finish:
                    i, L = finish
                    pe.wait_ge(s_at[L], i + 1)
                    transpose4(pe, ps[L][:, 2, :], attn[L][:], ident[:]).then_inc(s_t4[L], 1)
                if project:
                    i, L = project
                    pe.wait_ge(s_xn[L], i + 1)
                    transpose4(pe, ps[L][:, 1, :], xn[L][:], ident[:]).then_inc(s_t1[L], 1)
                if softmax:
                    i, L = softmax
                    scores(i, 1, L)
                if finish:
                    i, L = finish
                    pe.wait_ge(s_t4l[L], i + 1)
                    if isinstance(i, int) and i == 0 and L == 0:
                        pe.wait_ge(s_lo, len(pieces))
                    if cross:
                        pe.wait_ge(s_posd[L], i)
                    accumulate(3, i, L, aT[L], wo, slice(0, H)).then_inc(s_o[L], 1)
                if softmax:
                    i, L = softmax
                    scores(i, 2, L)
                    scores(i, 3, L)
                if project:
                    i, L = project
                    if starting:
                        pe.wait_ge(s_lo, FIRST_PIECES)
                    project_in(i, L, 0)
                if softmax and not cross:
                    i, L = softmax
                    probsT(i, 0, L)
                    probsT(i, 1, L)
                if project:
                    i, L = project
                    if starting:
                        pe.wait_ge(s_lo, 2 * FIRST_PIECES)
                    project_in(i, L, 1)
                    if starting:
                        pe.wait_ge(s_lo, 3 * FIRST_PIECES)
                    project_in(i, L, 2)
                if softmax and not cross:
                    i, L = softmax
                    probsT(i, 2, L)
                    probsT(i, 3, L)
                if project:
                    i, L = project
                    pe.wait_ge(s_qk[L], 2 * i + 2)
                    whole, parted = (k_sb, q_sb) if cross else (q_sb, k_sb)
                    if cross:
                        pe.wait_ge(s_of[L], i)
                    else:
                        pe.wait_ge(s_x1[L], i)
                    transpose4(pe, ps[L][:, 3, :], whole[L][:], ident[:]).then_inc(s_t2[L], 1)
                    transpose4(pe, ps[L][:, 0, :], parted[L][:], ident[:]).then_inc(s_t2[L], 1)
                if cross and finish:
                    i, L = finish
                    if project:
                        pe.wait_ge(s_v[L], i + 2)
                    route_turn(*finish)
                if softmax:
                    attend_v(*softmax)
                if cross and finish:
                    route_logits(*finish)
                if cross and route:
                    route_count(*route)

            if not cross:
                pe.wait_ge(s_ident, 1)
            pipeline(pe, half)


M, MCH = 352, ((0, 128), (128, 128), (256, 96))
HALF = CAP // 2
COLS = LANES * CAP // P
MS = 704
SCH = ((0, 128), (128, 128), (256, 128), (384, 128), (512, 96), (608, 96))
QT = 4


SHARED_LOADS = 16 * (2 + len(SCH))


def expert_phase(nc, wg_in, wu_in, wd_in, xf, table, y_out, ident, shared_in, shared_raw, shared_loaded):
    turns = E // 2
    with ExitStack() as ctx:
        def sb(name, shape, dt=F32):
            return ctx.enter_context(nc.sbuf_tensor("e_" + name, shape, dt))

        def pb(name):
            return ctx.enter_context(nc.psum_tensor("e_" + name, [P, 512], F32))

        sems = []

        def sem(name):
            sems.append(nc.alloc_semaphore("e_" + name))
            return sems[-1]

        def two(make, name, *a):
            return [make(f"{name}{b}", *a) for b in range(2)]

        names_row = sb("names_row", [E * CAP // P, P])
        names = sb("names", [P, E * CAP // P], U32)
        idx = sb("idx", [P, COLS], U32)
        carry = sb("carry", [P, 1])
        xones = sb("ones", [P, 1])
        xg = sb("xg", [P, COLS * H])
        xT = [sb("xT_hi", [P, KC, COLS * P], F32R), sb("xT_lo", [P, KC, COLS * P], F32R)]
        raw_g, raw_u = two(sb, "raw_g", [P, KC, M]), two(sb, "raw_u", [P, KC, M])
        raw_d = two(sb, "raw_d", [P, 3, H])
        wg, wu = ([two(sb, f"{n}_{b}", [P, KC, M], F32R) for b in range(2)] for n in ("wg", "wu"))
        wd = [two(sb, f"wd_{b}", [P, 3, H], F32R) for b in range(2)]
        act_g = two(sb, "act_g", [P, 3, CAP])
        h_raw = two(sb, "h_raw", [P, 3, CAP])
        hid = [two(sb, f"hid_{b}", [P, 3, CAP], F32R) for b in range(2)]
        y_sb = two(sb, "y", [HALF, 2, H])
        gu = [pb(f"gu{m}") for m in range(3)]
        dn = [pb(f"dn{h}") for h in range(2)]
        tr = [pb(f"tr{j}") for j in range(COLS)]

        s_row = sem("names_loaded")
        s_ones = sem("ones_ready")
        s_nT = sem("names_in_psum")
        s_names = sem("names_ready")
        s_idx = sem("idx_ready")
        s_x = [sem(f"tokens_gathered{j}") for j in range(COLS)]
        s_lg, s_lu, s_ld = two(sem, "wg_loaded"), two(sem, "wu_loaded"), two(sem, "wd_loaded")
        s_guh, s_gul = two(sem, "wgu_hi_ready"), two(sem, "wgu_lo_ready")
        s_dh, s_dl = two(sem, "wd_hi_ready"), two(sem, "wd_lo_ready")
        s_t = sem("xT_in_psum")
        s_th = sem("xT_hi_ready")
        s_tl = sem("xT_lo_ready")
        s_gu = sem("gate_up_in_psum")
        s_silu = sem("silu_ready")
        s_mul = sem("hidden_ready")
        s_hh = sem("hidden_hi_ready")
        s_hl = sem("hidden_lo_ready")
        s_dn = sem("down_in_psum")
        s_y = [sem("y_half0_ready"), sem("y_half1_ready")]
        s_st = two(sem, "y_stored")

        ctx.callback(end_phase, nc, sems)
        block = ctx.enter_context(nc.Block())

        def nxt(g, b):
            return (g, 1) if b == 0 else (g + 1, 0)

        def before(g, b, n):
            if isinstance(g, int) and 2 * g + b < n:
                return None
            if n == 1:
                return (g, 0) if b == 1 else (g - 1, 1)
            return (g - 1, b)

        @block.sync
        def _(sp):
            def load_gu(g, b, first):
                if not first:
                    sp.wait_ge(s_gul[b], 2 * g)
                rows = bass.ds((2 * g + b) * P, P)
                sp.dma_start(raw_g[b][:].rearrange("p k m -> p (k m)"), wg_in[rows, :]).then_inc(s_lg[b], 16)
                sp.dma_start(raw_u[b][:].rearrange("p k m -> p (k m)"), wu_in[rows, :]).then_inc(s_lu[b], 16)

            def load_d(g, b, first):
                if not first:
                    sp.wait_ge(s_dl[b], 2 * g)
                row = (2 * g + b) * M
                sp.dma_start(raw_d[b][:, 0:2, :], wd_in[bass.ds(row, 2 * P), :].rearrange("(c p) n -> p c n", p=P)
                             ).then_inc(s_ld[b], 16)
                sp.dma_start(raw_d[b][0:96, 2, :], wd_in[bass.ds(row + 2 * P, 96), :]).then_inc(s_ld[b], 16)

            def store(g, b):
                e = 2 * g + b
                sp.wait_ge(s_y[0], e + 1)
                sp.wait_ge(s_y[1], e + 1)
                sp.dma_start(y_out[bass.ds(e * CAP, CAP), :].rearrange("(f p) n -> p f n", p=HALF), y_sb[b][:]
                             ).then_inc(s_st[b], 16)

            sp.dma_start(names_row[:], table[0:SLOTS, :].rearrange("(c p) o -> c (p o)", p=P)).then_inc(s_row, 16)
            for b in range(2):
                load_gu(0, b, True)
                load_d(0, b, True)
            load_gu(1, 0, False)
            for src, dst in zip(shared_in[0:2], shared_raw[0:2]):
                sp.dma_start(dst[:], src.rearrange("(k p) m -> p k m", p=P)).then_inc(shared_loaded, 16)
            for c, (m, n) in enumerate(SCH):
                sp.dma_start(shared_raw[2][0:n, c, :], shared_in[2][m:m + n, :]).then_inc(shared_loaded, 16)

            def turn(g, first, last):
                if not last:
                    if not first:
                        load_gu(g + 1, 0, False)
                    load_gu(g + 1, 1, False)
                    load_d(g + 1, 0, False)
                if not first:
                    store(g - 1, 0)
                    store(g - 1, 1)
                if not last:
                    load_d(g + 1, 1, False)

            turn(0, True, False)
            with sp.Fori(1, turns - 1) as g:
                turn(g, False, False)
            turn(turns - 1, False, True)
            for b in range(2):
                store(turns - 1, b)
            for b in range(2):
                sp.wait_ge(s_st[b], 16 * turns)

        @block.gpsimd
        def _(pool):
            def gather(g, first):
                if not first:
                    pool.wait_ge(s_t, COLS * g)
                pool.tensor_copy(idx[:], names[:, bass.ds(g * COLS, COLS)]).then_inc(s_idx, 1)
                pool.wait_ge(s_idx, g + 1)
                if not isinstance(g, int):
                    pool.tensor_tensor(carry[:], xones[:], xones[:], ALU.mult)
                for j in range(COLS):
                    pool.indirect_dma_start(out=xg[:, j * H:(j + 1) * H], out_offset=None, in_=xf,
                                            in_offset=bass.IndirectOffsetOnAxis(ap=idx[:, j:j + 1], axis=0)
                                            ).then_inc(s_x[j], 16)

            def hidden_lo(g, b):
                for c, (_, n) in enumerate(MCH):
                    e = 2 * g + b
                    pool.wait_ge(s_hh, 3 * e + c + 1)
                    f = before(g, b, 2)
                    if f is not None:
                        pool.wait_ge(s_dn, 2 * (2 * f[0] + b) + 2)
                    pool.tensor_tensor(hid[b][1][0:n, c, :], h_raw[b][0:n, c, :], hid[b][0][0:n, c, :].bitcast(F32),
                                       ALU.subtract).then_inc(s_hl, 1)

            pool.memset(xones[:], 1.0).then_inc(s_ones, 1)
            pool.wait_ge(s_ones, 1)
            pool.wait_ge(s_names, 1)
            gather(0, True)

            def turn(g, last):
                if not last:
                    gather(g + 1, False)
                for b in range(2):
                    hidden_lo(g, b)

            turn(0, False)
            with pool.Fori(1, turns - 1) as g:
                turn(g, False)
            turn(turns - 1, True)

        @block.scalar
        def _(act):
            def gu_hi(g, b, which):
                raw, w, s = ((raw_g, wg, s_lg), (raw_u, wu, s_lu))[which]
                act.wait_ge(s[b], 16 * (g + 1))
                f = before(g, b, 2)
                if f is not None:
                    act.wait_ge(s_mul, 3 * (2 * f[0] + b) + 3)
                act.activation(w[b][0][:], raw[b][:], ACT.Copy).then_inc(s_guh[b], 1)

            def d_hi(g, b, part):
                if part == 0:
                    act.wait_ge(s_ld[b], 32 * (g + 1))
                f = before(g, b, 2)
                if f is not None:
                    act.wait_ge(s_dn, 2 * (2 * f[0] + b) + 2)
                rows, cs = ((P, slice(0, 2)), (96, slice(2, 3)))[part]
                act.activation(wd[b][0][0:rows, cs, :], raw_d[b][0:rows, cs, :], ACT.Copy).then_inc(s_dh[b], 1)

            def silu(g, b, c):
                n = MCH[c][1]
                act.wait_ge(s_gu, 3 * (2 * g + b) + c + 1)
                act.activation(act_g[b][0:n, c, :], gu[c][0:n, 0:CAP], ACT.Silu).then_inc(s_silu, 1)

            def hidden_hi(g, b, c):
                n = MCH[c][1]
                act.wait_ge(s_mul, 3 * (2 * g + b) + c + 1)
                act.activation(hid[b][0][0:n, c, :], h_raw[b][0:n, c, :], ACT.Copy).then_inc(s_hh, 1)

            def x_hi(g):
                for j in range(COLS):
                    act.wait_ge(s_t, COLS * g + j + 1)
                    act.activation(xT[0][:, :, j * P:(j + 1) * P], tr[j][:].rearrange("p (k s) -> p k s", k=KC),
                                   ACT.Copy).then_inc(s_th, 1)

            def y_half(g, b):
                act.wait_ge(s_dn, 2 * (2 * g + b) + 1)
                if not (isinstance(g, int) and g == 0):
                    act.wait_ge(s_st[b], 16 * g)
                act.activation(y_sb[b][:, 0, :], dn[0][0:HALF, :], ACT.Copy).then_inc(s_y[0], 1)

            def half(g, b, last):
                f = before(g, b, 2)
                if f is not None:
                    y_half(*f)
                more = not (last and b == 1)
                if more:
                    gu_hi(*nxt(g, b), 0)
                silu(g, b, 0)
                if more:
                    gu_hi(*nxt(g, b), 1)
                hidden_hi(g, b, 0)
                silu(g, b, 1)
                d_hi(g, b, 0)
                hidden_hi(g, b, 1)
                silu(g, b, 2)
                d_hi(g, b, 1)
                hidden_hi(g, b, 2)
                if b == 1 and not last:
                    x_hi(g + 1)

            gu_hi(0, 0, 0)
            gu_hi(0, 0, 1)
            x_hi(0)
            for b in range(2):
                half(0, b, False)
            with act.Fori(1, turns - 1) as g:
                for b in range(2):
                    half(g, b, False)
            for b in range(2):
                half(turns - 1, b, True)
            for b in range(2):
                y_half(turns - 1, b)

        @block.vector
        def _(dve):
            def gu_lo(g, b, which):
                raw, w = ((raw_g, wg), (raw_u, wu))[which]
                dve.wait_ge(s_guh[b], 2 * g + which + 1)
                dve.tensor_tensor(w[b][1][:], raw[b][:], w[b][0][:].bitcast(F32), ALU.subtract).then_inc(s_gul[b], 1)

            def d_lo(g, b, part):
                dve.wait_ge(s_dh[b], 2 * g + part + 1)
                rows, cs = ((P, slice(0, 2)), (96, slice(2, 3)))[part]
                dve.tensor_tensor(wd[b][1][0:rows, cs, :], raw_d[b][0:rows, cs, :], wd[b][0][0:rows, cs, :].bitcast(F32),
                                  ALU.subtract).then_inc(s_dl[b], 1)

            def hidden(g, b, c):
                n, e = MCH[c][1], 2 * g + b
                dve.wait_ge(s_silu, 3 * e + c + 1)
                f = before(g, b, 2)
                if f is not None:
                    dve.wait_ge(s_hl, 3 * (2 * f[0] + b) + c + 1)
                dve.tensor_tensor(h_raw[b][0:n, c, :], gu[c][0:n, CAP:2 * CAP], act_g[b][0:n, c, :], ALU.mult).then_inc(s_mul, 1)

            def x_lo(g):
                for j in range(COLS):
                    dve.wait_ge(s_th, COLS * g + j + 1)
                    cols = slice(j * P, (j + 1) * P)
                    dve.tensor_tensor(xT[1][:, :, cols], tr[j][:].rearrange("p (k s) -> p k s", k=KC),
                                      xT[0][:, :, cols].bitcast(F32), ALU.subtract).then_inc(s_tl, 1)

            def y_half(g, b):
                dve.wait_ge(s_dn, 2 * (2 * g + b) + 2)
                if not (isinstance(g, int) and g == 0):
                    dve.wait_ge(s_st[b], 16 * g)
                dve.tensor_copy(y_sb[b][:, 1, :], dn[1][0:HALF, :]).then_inc(s_y[1], 1)

            def half(g, b, last):
                f = before(g, b, 2)
                if f is not None:
                    y_half(*f)
                more = not (last and b == 1)
                if more:
                    gu_lo(*nxt(g, b), 0)
                hidden(g, b, 0)
                if more:
                    gu_lo(*nxt(g, b), 1)
                hidden(g, b, 1)
                d_lo(g, b, 0)
                hidden(g, b, 2)
                d_lo(g, b, 1)
                if b == 1 and not last:
                    x_lo(g + 1)

            dve.wait_ge(s_nT, 1)
            dve.tensor_copy(names[:], gu[0][:, 0:E * CAP // P]).then_inc(s_names, 1)
            gu_lo(0, 0, 0)
            gu_lo(0, 0, 1)
            x_lo(0)
            for b in range(2):
                half(0, b, False)
            with dve.Fori(1, turns - 1) as g:
                for b in range(2):
                    half(g, b, False)
            for b in range(2):
                half(turns - 1, b, True)
            for b in range(2):
                y_half(turns - 1, b)

        @block.tensor
        def _(pe):
            def turn_tokens(g):
                for j in range(COLS):
                    pe.wait_ge(s_x[j], 16 * (g + 1))
                    transpose4(pe, tr[j], xg[:, j * H:(j + 1) * H], ident[:]).then_inc(s_t, 1)

            def gate_up(g, b):
                e = 2 * g + b
                if b == 0:
                    pe.wait_ge(s_tl, COLS * (g + 1))
                pe.wait_ge(s_gul[b], 2 * (g + 1))
                toks = slice(b * CAP, (b + 1) * CAP)
                for c, (m, n) in enumerate(MCH):
                    f = before(g, b, 1)
                    if f is not None:
                        pe.wait_ge(s_mul, 3 * (2 * f[0] + f[1]) + c + 1)
                    for w, at in ((wg, 0), (wu, CAP)):
                        for k in range(KC):
                            ins = matmul3(pe, gu[c][0:n, at:at + CAP], (w[b][0][:, k, m:m + n], w[b][1][:, k, m:m + n]),
                                          (xT[0][:, k, toks], xT[1][:, k, toks]), k == 0, k == KC - 1)
                    ins.then_inc(s_gu, 1)

            def down(g, b):
                e = 2 * g + b
                pe.wait_ge(s_dl[b], 2 * (g + 1))
                pe.wait_ge(s_hl, 3 * e + 3)
                f = before(g, b, 1)
                for hf in range(2):
                    if f is not None:
                        pe.wait_ge(s_y[hf], 2 * f[0] + f[1] + 1)
                    toks = slice(hf * HALF, (hf + 1) * HALF)
                    for c, (_, n) in enumerate(MCH):
                        ins = matmul3(pe, dn[hf][0:HALF, :], (hid[b][0][0:n, c, toks], hid[b][1][0:n, c, toks]),
                                      (wd[b][0][0:n, c, :], wd[b][1][0:n, c, :]), c == 0, c == 2)
                    ins.then_inc(s_dn, 1)

            pe.wait_ge(s_row, 16)
            pe.transpose(gu[0][:, 0:E * CAP // P], names_row[:], ident[0:E * CAP // P, 0:E * CAP // P]).then_inc(s_nT, 1)
            turn_tokens(0)
            pe.wait_ge(s_names, 1)

            def turn(g, last):
                gate_up(g, 0)
                f = before(g, 0, 1)
                if f is not None:
                    down(*f)
                gate_up(g, 1)
                if not last:
                    turn_tokens(g + 1)
                down(g, 0)

            turn(0, False)
            with pe.Fori(1, turns - 1) as g:
                turn(g, False)
            turn(turns - 1, True)
            down(turns - 1, 1)


def shared_phase(nc, raw, loaded, xf, x3, y_in, out, weight, slot, ident):
    quads = BATCH // QT
    with ExitStack() as ctx:
        def sb(name, shape, dt=F32):
            return ctx.enter_context(nc.sbuf_tensor("h_" + name, shape, dt))

        def pb(name):
            return ctx.enter_context(nc.psum_tensor("h_" + name, [P, 512], F32))

        sems = []

        def sem(name):
            sems.append(nc.alloc_semaphore("h_" + name))
            return sems[-1]

        def two(make, name, *a):
            return [make(f"{name}{b}", *a) for b in range(2)]

        sg, su = two(sb, "sg_", [P, KC, MS], F32R), two(sb, "su_", [P, KC, MS], F32R)
        sd = two(sb, "sd_", [P, len(SCH), H], F32R)
        xf_sb = sb("xf", [P, QT, H])
        xT = two(sb, "xT_", [P, KC, QT * P], F32R)
        act_g = two(sb, "act_g", [P, QT * P])
        h_raw = two(sb, "h_raw", [P, QT * P])
        hid = two(sb, "hid_", [P, len(SCH), QT * P], F32R)
        yk = two(sb, "yk", [P, TOPK * H])
        acc = two(sb, "acc", [P, H])
        o_sb = two(sb, "o", [P, H])
        idx = two(sb, "idx", [P, TOPK], U32)
        w_t = two(sb, "w_t", [P, TOPK])
        carry = two(sb, "carry", [P, 1])
        ones = sb("ones", [P, 1])
        tr, gt, up, dn = two(pb, "tr"), two(pb, "gt"), two(pb, "up"), two(pb, "dn")

        s_wh, s_wl = sem("weight_hi"), sem("weight_lo")
        s_xf = sem("xf_loaded")
        s_t, s_th, s_tl = sem("xT_in_psum"), sem("xT_hi_ready"), sem("xT_lo_ready")
        s_gu, s_silu, s_mul = sem("gate_up_in_psum"), sem("silu_ready"), sem("hidden_ready")
        s_hh, s_hl = sem("hidden_hi_ready"), sem("hidden_lo_ready")
        s_dn = sem("down_in_psum")
        s_x3 = two(sem, "x3_loaded")
        s_idx = two(sem, "idx_ready")
        s_yk = [[sem(f"rows_gathered{b}_{k}") for k in range(TOPK)] for b in range(2)]
        s_wt = two(sem, "weights_ready")
        s_acc = two(sem, "routed_sum_step")
        s_o = two(sem, "out_ready")
        s_st = two(sem, "out_stored")
        s_ones = sem("ones_ready")

        raw_g, raw_u, raw_d = raw
        pieces = []
        for k in range(KC):
            for src, w in ((raw_g, sg), (raw_u, su)):
                pieces.append((src[:, k, :], [d[:, k, :] for d in w]))
        in_pieces = len(pieces)
        for c, (_, n) in enumerate(SCH):
            pieces.append((raw_d[0:n, c, :], [d[0:n, c, :] for d in sd]))

        ctx.callback(end_phase, nc, sems)
        block = ctx.enter_context(nc.Block())
        per_tile = 1 + TOPK

        @block.sync
        def _(sp):
            def load_xf(q):
                sp.dma_start(xf_sb[:], xf[bass.ds(q * QT * P, QT * P), :].rearrange("(t p) h -> p t h", p=P)).then_inc(s_xf, 16)

            def load_x3(q, t, first):
                b = t % 2
                if not first:
                    sp.wait_ge(s_o[b], q * (QT // 2) + t // 2)
                sp.dma_start(acc[b][:], x3[bass.ds((q * QT + t) * P, P), :]).then_inc(s_x3[b], 16)

            def store(q, t):
                b = t % 2
                sp.wait_ge(s_o[b], q * (QT // 2) + t // 2 + 1)
                sp.dma_start(out[bass.ds((q * QT + t) * P, P), :], o_sb[b][:]).then_inc(s_st[b], 16)

            load_xf(0)
            for t in range(2):
                load_x3(0, t, True)

            def turn(q, last):
                if not last:
                    sp.wait_ge(s_t, QT * (q + 1))
                    load_xf(q + 1)
                for t in range(QT):
                    store(q, t)
                    if not (last and t >= QT - 2):
                        nq, nt = (q, t + 2) if t + 2 < QT else (q + 1, t + 2 - QT)
                        load_x3(nq, nt, False)

            with sp.Fori(0, quads - 1) as q:
                turn(q, False)
            turn(quads - 1, True)
            for b in range(2):
                sp.wait_ge(s_st[b], 16 * BATCH // 2)

        @block.gpsimd
        def _(pool):
            pool.memset(ones[:], 1.0).then_inc(s_ones, 1)
            pool.wait_ge(s_ones, 1)

            def gather(q, t, first):
                b = t % 2
                n = q * (QT // 2) + t // 2
                if not first:
                    pool.wait_ge(s_acc[b], TOPK * n)
                pool.tensor_copy(idx[b][:], slot[:, bass.ds((q * QT + t) * TOPK, TOPK)]).then_inc(s_idx[b], 1)
                pool.wait_ge(s_idx[b], n + 1)
                if not isinstance(q, int):
                    pool.tensor_tensor(carry[b][:], ones[:], ones[:], ALU.mult)
                for k in range(TOPK):
                    pool.indirect_dma_start(out=yk[b][:, k * H:(k + 1) * H], out_offset=None, in_=y_in,
                                            in_offset=bass.IndirectOffsetOnAxis(ap=idx[b][:, k:k + 1], axis=0)
                                            ).then_inc(s_yk[b][k], 16)

            for t in range(QT):
                gather(0, t, t < 2)
            with pool.Fori(1, quads) as q:
                for t in range(QT):
                    gather(q, t, False)

        @block.scalar
        def _(act):
            def split_weights(a, b):
                for src, dst in pieces[a:b]:
                    act.activation(dst[0], src, ACT.Copy).then_inc(s_wh, 1)

            def x_hi(q):
                for t in range(QT):
                    act.wait_ge(s_t, QT * q + t + 1)
                    act.activation(xT[0][:, :, t * P:(t + 1) * P], tr[t % 2][:].rearrange("p (k s) -> p k s", k=KC),
                                   ACT.Copy).then_inc(s_th, 1)

            def hidden_hi(q, c):
                n = SCH[c][1]
                act.wait_ge(s_mul, len(SCH) * q + c + 1)
                act.activation(hid[0][0:n, c, :], h_raw[c % 2][0:n, :], ACT.Copy).then_inc(s_hh, 1)

            def turn(q, last):
                for c, (_, n) in enumerate(SCH):
                    act.wait_ge(s_gu, len(SCH) * q + c + 1)
                    act.activation(act_g[c % 2][0:n, :], gt[c % 2][0:n, :], ACT.Silu).then_inc(s_silu, 1)
                    if c:
                        hidden_hi(q, c - 1)
                hidden_hi(q, len(SCH) - 1)
                if not last:
                    x_hi(q + 1)

            act.wait_ge(loaded, SHARED_LOADS)
            split_weights(0, in_pieces)
            x_hi(0)
            split_weights(in_pieces, len(pieces))
            with act.Fori(0, quads - 1) as q:
                turn(q, False)
            turn(quads - 1, True)

        @block.vector
        def _(dve):
            def split_weights(a, b):
                for n in range(a, b):
                    src, dst = pieces[n]
                    dve.wait_ge(s_wh, n + 1)
                    dve.tensor_tensor(dst[1], src, dst[0].bitcast(F32), ALU.subtract).then_inc(s_wl, 1)

            def x_lo(q):
                for t in range(QT):
                    cols = slice(t * P, (t + 1) * P)
                    dve.wait_ge(s_th, QT * q + t + 1)
                    dve.tensor_tensor(xT[1][:, :, cols], tr[t % 2][:].rearrange("p (k s) -> p k s", k=KC),
                                      xT[0][:, :, cols].bitcast(F32), ALU.subtract).then_inc(s_tl, 1)

            def routed(q, t):
                b = t % 2
                n = q * (QT // 2) + t // 2
                dve.wait_ge(s_x3[b], 16 * (n + 1))
                dve.tensor_copy(w_t[b][:], weight[:, bass.ds((q * QT + t) * TOPK, TOPK)]).then_inc(s_wt[b], 1)
                dve.wait_ge(s_wt[b], n + 1)
                for k in range(TOPK):
                    dve.wait_ge(s_yk[b][k], 16 * (n + 1))
                    dve.scalar_tensor_tensor(acc[b][:], yk[b][:, k * H:(k + 1) * H], w_t[b][:, k:k + 1], acc[b][:],
                                             ALU.mult, ALU.add).then_inc(s_acc[b], 1)
                    dve.wait_ge(s_acc[b], TOPK * n + k + 1)

            def finish(q, t, first):
                b = t % 2
                n = q * (QT // 2) + t // 2
                dve.wait_ge(s_dn, QT * q + t + 1)
                if not first:
                    dve.wait_ge(s_st[b], 16 * n)
                dve.tensor_tensor(o_sb[b][:], dn[b][:], acc[b][:], ALU.add).then_inc(s_o[b], 1)

            def turn(q, first, last):
                for c, (_, n) in enumerate(SCH):
                    dve.wait_ge(s_silu, len(SCH) * q + c + 1)
                    if not (first and c < 2):
                        dve.wait_ge(s_hl, len(SCH) * q + c - 1)
                    dve.tensor_tensor(h_raw[c % 2][0:n, :], up[c % 2][0:n, :], act_g[c % 2][0:n, :], ALU.mult).then_inc(s_mul, 1)
                    if c >= 1:
                        hidden_lo(q, c - 1, first)
                hidden_lo(q, len(SCH) - 1, first)
                if not last:
                    x_lo(q + 1)
                for t in range(QT):
                    routed(q, t)
                    finish(q, t, first and t < 2)

            def hidden_lo(q, c, first):
                n = SCH[c][1]
                dve.wait_ge(s_hh, len(SCH) * q + c + 1)
                dve.tensor_tensor(hid[1][0:n, c, :], h_raw[c % 2][0:n, :], hid[0][0:n, c, :].bitcast(F32),
                                  ALU.subtract).then_inc(s_hl, 1)

            split_weights(0, in_pieces)
            x_lo(0)
            split_weights(in_pieces, len(pieces))
            turn(0, True, False)
            with dve.Fori(1, quads - 1) as q:
                turn(q, False, False)
            turn(quads - 1, False, True)

        @block.tensor
        def _(pe):
            def turn_tokens(q, first):
                for t in range(QT):
                    if t == 0:
                        pe.wait_ge(s_xf, 16 * (q + 1))
                    if t >= 2:
                        pe.wait_ge(s_tl, QT * q + t - 1)
                    transpose4(pe, tr[t % 2], xf_sb[:, t, :], ident[:]).then_inc(s_t, 1)

            def hidden(q, first):
                pe.wait_ge(s_tl, QT * (q + 1))
                for c, (m, n) in enumerate(SCH):
                    if not (first and c < 2):
                        pe.wait_ge(s_mul, len(SCH) * q + c - 1)
                    for w, bank in ((sg, gt[c % 2]), (su, up[c % 2])):
                        for k in range(KC):
                            ins = matmul3(pe, bank[0:n, :], (w[0][:, k, m:m + n], w[1][:, k, m:m + n]),
                                          (xT[0][:, k, :], xT[1][:, k, :]), k == 0, k == KC - 1)
                    ins.then_inc(s_gu, 1)

            def down(q, first):
                pe.wait_ge(s_hl, len(SCH) * (q + 1))
                for t in range(QT):
                    if not (first and t < 2):
                        pe.wait_ge(s_o[t % 2], q * (QT // 2) + t // 2)
                    toks = slice(t * P, (t + 1) * P)
                    for c, (_, n) in enumerate(SCH):
                        ins = matmul3(pe, dn[t % 2][:], (hid[0][0:n, c, toks], hid[1][0:n, c, toks]),
                                      (sd[0][0:n, c, :], sd[1][0:n, c, :]), c == 0, c == len(SCH) - 1)
                    ins.then_inc(s_dn, 1)

            turn_tokens(0, True)
            pe.wait_ge(s_wl, in_pieces)

            def turn(q, first, last):
                hidden(q, first)
                if not last:
                    turn_tokens(q + 1, False)
                if first:
                    pe.wait_ge(s_wl, len(pieces))
                down(q, first)

            turn(0, True, False)
            with pe.Fori(1, quads - 1) as q:
                turn(q, False, False)
            turn(quads - 1, False, True)


_INS = ['x', 'ctx_2048', 'mask_BxS2_ik0', 'L0_attn_Wqkv', 'L0_attn_bqkv', 'L0_attn_Wo', 'L0_attn_bo', 'L0_xattn_Wq',
        'L0_xattn_bq', 'L0_xattn_Wk', 'L0_xattn_bk', 'L0_xattn_Wv', 'L0_xattn_bv', 'L0_xattn_Wo', 'L0_xattn_bo',
        'L0_xattn_ln_gamma', 'L0_xattn_ln_beta', 'L0_xattn_residual_scale', 'L0_ffn_gate_weight', 'L0_ffn_Wg',
        'L0_ffn_Wu', 'L0_ffn_Wd', 'L0_ffn_Sg', 'L0_ffn_Su', 'L0_ffn_Sd']


def _lay(name, a):
    if name == 'x':
        return a.reshape(T, H)
    if name == 'ctx_2048':
        return a.transpose(0, 2, 1).reshape(BATCH, KC, P, SEQ).transpose(0, 2, 1, 3).reshape(T, H)
    if name == 'mask_BxS2_ik0':
        return a.T
    if name == 'L0_xattn_residual_scale':
        return a.reshape(1)
    if name in ('L0_ffn_Wg', 'L0_ffn_Wu'):
        return a.transpose(0, 2, 1).reshape(E, KC, P, M).transpose(0, 2, 1, 3).reshape(E * P, KC * M)
    if name == 'L0_ffn_Wd':
        return a.transpose(0, 2, 1).reshape(E * M, H)
    if name.startswith('L0_xattn_W') or name.startswith('L0_ffn'):
        return a.T
    return a


def build(nc, a, out):
    with ExitStack() as ctx:
        ident = ctx.enter_context(nc.sbuf_tensor("ident", [P, P], F32))
        weight = ctx.enter_context(nc.sbuf_tensor("weight", [P, BATCH * TOPK], F32))
        slot = ctx.enter_context(nc.sbuf_tensor("slot", [P, BATCH * TOPK], U32))
        x1 = nc.dram_tensor("x1_dram", [T, H], F32, kind="Internal").ap()
        x3 = nc.dram_tensor("x3_dram", [T, H], F32, kind="Internal").ap()
        xf = nc.dram_tensor("xf_dram", [T, H], F32, kind="Internal").ap()
        table = nc.dram_tensor("table_dram", [2 * SLOTS, 1], F32, kind="Internal").ap()
        y = nc.dram_tensor("y_dram", [SLOTS, H], F32, kind="Internal").ap()
        const = dict(ident=ident)
        n = 'L0_xattn_'
        self_pieces = weight_pieces([a['L0_attn_Wqkv']], [a['L0_attn_Wo']])
        cross_pieces = weight_pieces([a[n + 'Wq'], a[n + 'Wk'], a[n + 'Wv']],
                                     [a[n + 'Wo'], a['L0_ffn_gate_weight']])
        early = nc.alloc_semaphore("next_weights_loaded")
        with nc.sbuf_tensor("stage", [P, STAGES, H], F32) as stage:
            attention_phase(nc, False, a['x'], None, self_pieces, [a['L0_attn_bqkv'], a['L0_attn_bo']], x1,
                            stage, None, const=const, ahead=(cross_pieces, early))
            attention_phase(nc, True, x1, a['ctx_2048'], cross_pieces,
                            [a[n + k] for k in ('bq', 'bk', 'bv', 'bo', 'ln_gamma', 'ln_beta', 'residual_scale')], x3,
                            stage, early, route=dict(mask=a['mask_BxS2_ik0'], xf=xf, table=table,
                                                     weight=weight, slot=slot), const=const)
        shared_loaded = nc.alloc_semaphore("shared_weights_loaded")
        with ExitStack() as kept:
            shared_raw = [kept.enter_context(nc.sbuf_tensor(name, shape, F32)) for name, shape in
                          (("raw_sg", [P, KC, MS]), ("raw_su", [P, KC, MS]), ("raw_sd", [P, len(SCH), H]))]
            expert_phase(nc, a['L0_ffn_Wg'], a['L0_ffn_Wu'], a['L0_ffn_Wd'], xf, table, y, ident,
                         [a['L0_ffn_Sg'], a['L0_ffn_Su'], a['L0_ffn_Sd']], shared_raw, shared_loaded)
            shared_phase(nc, shared_raw, shared_loaded, xf, x3, y, out, weight, slot, ident)


def kernel(**inputs):
    import numpy as _np
    import concourse.bacc as _bacc
    from concourse import mybir as _mybir
    from concourse.bass_utils import run_bass_kernel_spmd as _run

    nc = _bacc.Bacc("TRN2", target_bir_lowering=False, num_devices=1)
    arrays, args = {}, {}
    for name in _INS:
        a = _np.ascontiguousarray(_lay(name, _np.asarray(inputs[name])))
        arrays[f"in_{name}_dram"] = a
        args[name] = nc.dram_tensor(f"in_{name}_dram", a.shape, _mybir.dt.from_np(a.dtype), kind="ExternalInput").ap()
    out = nc.dram_tensor("out_0_dram", (T, H), _mybir.dt.from_np(_np.dtype('float32')), kind="ExternalOutput").ap()
    build(nc, args, out)
    r = _run(nc, [arrays], core_ids=[0])
    return r.results[0]["out_0_dram"].reshape(BATCH, SEQ, H)
```
